# Optimizing a Trainium2 kernel written in Bass

```python
import numpy as np
import jax
import jax.numpy as jnp

def _softmax(x, axis=-1):
    return jax.nn.softmax(x, axis=axis)

def _gelu(x):
    return jax.nn.gelu(x, approximate=True)

def _silu(x):
    return jax.nn.silu(x)

def _sigmoid(x):
    return jax.nn.sigmoid(x)

def _layernorm(x, axis=-1, eps=1e-05):
    m = jnp.mean(x, axis=axis, keepdims=True)
    v = jnp.var(x, axis=axis, keepdims=True)
    return (x - m) / jnp.sqrt(v + eps)

def _scatter_add(tgt, idx, src, axis=0):
    return tgt.at[idx].add(src)

def _segment_sum(src, seg, n):
    return jax.ops.segment_sum(src, seg, n)
kernel_name = 'mk_metaformer_d1_conv_nchw512_r4_9ae4a3'

def setup_inputs(seed: int=0):
    np.random.seed(seed)
    _w = jnp.asarray

    def _rec_inputs():
        import jax
        import jax.numpy as jnp
        _gk = jax.random.key(seed)
        x = -0.0003482 + 1 * jax.random.normal(jax.random.fold_in(_gk, 1), (16, 128, 48, 48), jnp.float32)
        return x
    x = _rec_inputs()

    def _L0_conv_setup():
        import jax, jax.numpy as jnp
        import numpy as np
        LN_EPS = 1e-05

        def layernorm(x, w, b, eps=LN_EPS):
            m = jnp.mean(x, -1, keepdims=True)
            v = jnp.mean(jnp.square(x - m), -1, keepdims=True)
            return (x - m) * jax.lax.rsqrt(v + eps) * w + b

        def to_seq(x, k):
            B, d, H, W = x.shape
            if k >= 2:
                x = jnp.swapaxes(x, 2, 3)
            s = x.reshape(B, d, H * W)
            if k % 2 == 1:
                s = s[:, :, ::-1]
            return s

        def from_seq(y, k, H, W):
            B, d, L = y.shape
            if k % 2 == 1:
                y = y[:, :, ::-1]
            if k >= 2:
                y = jnp.swapaxes(y.reshape(B, d, W, H), 2, 3)
            else:
                y = y.reshape(B, d, H, W)
            return y

        def ss2d(x, k, Win, cw, cb, Wx, Wdt, dtb, A_log, Dp, nw, nb, Wout):
            B, H, W, d = x.shape
            xz = x @ Win
            xin, z = jnp.split(xz, 2, axis=-1)
            xc = jnp.transpose(xin, (0, 3, 1, 2))
            xc = jax.lax.conv_general_dilated(xc, cw, (1, 1), ((1, 1), (1, 1)), feature_group_count=d) + cb[None, :, None, None]
            xc = jax.nn.silu(xc)
            u = to_seq(xc, k)
            x_dbl = jnp.einsum('bdl,rd->brl', u, Wx)
            dtr = Wdt.shape[1]
            N = A_log.shape[1]
            dt, Bm, Cm = jnp.split(x_dbl, [dtr, dtr + N], axis=1)
            delta = jax.nn.softplus(jnp.einsum('brl,dr->bdl', dt, Wdt) + dtb[None, :, None])
            A = -jnp.exp(A_log)
            dA = jnp.exp(delta[..., None] * A[None, :, None, :])
            dBu = (delta * u)[..., None] * jnp.transpose(Bm, (0, 2, 1))[:, None]

            def comb(c1, c2):
                a1, b1 = c1
                a2, b2 = c2
                return (a1 * a2, a2 * b1 + b2)
            _, h = jax.lax.associative_scan(comb, (dA, dBu), axis=2)
            y = jnp.einsum('bdln,bnl->bdl', h, Cm) + Dp[:, None] * u
            y = jnp.transpose(from_seq(y, k, H, W), (0, 2, 3, 1))
            y = layernorm(y, nw, nb)
            y = y * jax.nn.silu(z)
            return y @ Wout
        key = jax.random.key(seed)
        ks = jax.random.split(key, 12)
        B, C, H, W = (16, 128, 48, 48)
        d, N, dtr, red = (C // 4, 1, 8, C // 16)

        def rn(k, shp, s=0.02):
            return (jax.random.normal(k, shp) * s).astype(jnp.float32)
        return {'x': jax.random.normal(ks[0], (B, C, H, W), jnp.float32), 'norm_w': jnp.ones((C,), jnp.float32), 'norm_b': jnp.zeros((C,), jnp.float32), 'fc1_w': rn(ks[1], (C, red)), 'fc1_b': jnp.zeros((red,), jnp.float32), 'fc2_w': rn(ks[2], (red, C)), 'fc2_b': jnp.zeros((C,), jnp.float32), 'Win': rn(ks[3], (4, d, 2 * d)), 'conv_w': rn(ks[4], (4, d, 1, 3, 3), 0.1), 'conv_b': jnp.zeros((4, d), jnp.float32), 'Wx': rn(ks[5], (4, dtr + 2 * N, d)), 'Wdt': rn(ks[6], (4, d, dtr), 0.1), 'dt_bias': jnp.full((4, d), -4.6, jnp.float32), 'A_log': jnp.zeros((4, d, N), jnp.float32), 'Dp': jnp.ones((4, d), jnp.float32), 'onorm_w': jnp.ones((4, d), jnp.float32), 'onorm_b': jnp.zeros((4, d), jnp.float32), 'Wout': rn(ks[7], (4, d, d)), 'proj_w': rn(ks[8], (C, C)), 'proj_b': jnp.zeros((C,), jnp.float32), 'skip_scale': jnp.ones((1,), jnp.float32)}
    _L0_conv_all = _L0_conv_setup()
    _L0_conv_in = {k: v for k, v in _L0_conv_all.items() if k in ('norm_w', 'norm_b', 'fc1_w', 'fc1_b', 'fc2_w', 'fc2_b', 'Win', 'conv_w', 'conv_b', 'Wx', 'Wdt', 'dt_bias', 'A_log', 'Dp', 'onorm_w', 'onorm_b', 'Wout', 'proj_w', 'proj_b', 'skip_scale')}
    del _L0_conv_all

    def _L0_ffn_setup():
        import jax, jax.numpy as jnp
        import numpy as np
        B, S, D = (8, 2048, 128)
        E, DFF = (16, 128)
        CAPACITY = 2
        key = jax.random.key(seed)
        ks = jax.random.split(key, 4)
        x = jax.random.normal(ks[0], (B, S, D), dtype=jnp.float32)
        gate_weight = jax.random.normal(ks[1], (D, E), dtype=jnp.float32) * 0.006
        w1 = jax.random.normal(ks[2], (E, D, DFF), dtype=jnp.float32) * 0.02
        b1 = jnp.zeros((E, DFF), dtype=jnp.float32)
        w2 = jax.random.normal(ks[3], (E, DFF, D), dtype=jnp.float32) * 0.02
        b2 = jnp.zeros((E, D), dtype=jnp.float32)
        return {'x': x, 'gate_weight': gate_weight, 'w1': w1, 'b1': b1, 'w2': w2, 'b2': b2}
    _L0_ffn_all = _L0_ffn_setup()
    _L0_ffn_in = {k: v for k, v in _L0_ffn_all.items() if k in ('gate_weight', 'w1', 'b1', 'w2', 'b2')}
    del _L0_ffn_all
    return {'x': x, 'L0_conv_norm_w': _L0_conv_in['norm_w'], 'L0_conv_norm_b': _L0_conv_in['norm_b'], 'L0_conv_fc1_w': _L0_conv_in['fc1_w'], 'L0_conv_fc1_b': _L0_conv_in['fc1_b'], 'L0_conv_fc2_w': _L0_conv_in['fc2_w'], 'L0_conv_fc2_b': _L0_conv_in['fc2_b'], 'L0_conv_Win': _L0_conv_in['Win'], 'L0_conv_conv_w': _L0_conv_in['conv_w'], 'L0_conv_conv_b': _L0_conv_in['conv_b'], 'L0_conv_Wx': _L0_conv_in['Wx'], 'L0_conv_Wdt': _L0_conv_in['Wdt'], 'L0_conv_dt_bias': _L0_conv_in['dt_bias'], 'L0_conv_A_log': _L0_conv_in['A_log'], 'L0_conv_Dp': _L0_conv_in['Dp'], 'L0_conv_onorm_w': _L0_conv_in['onorm_w'], 'L0_conv_onorm_b': _L0_conv_in['onorm_b'], 'L0_conv_Wout': _L0_conv_in['Wout'], 'L0_conv_proj_w': _L0_conv_in['proj_w'], 'L0_conv_proj_b': _L0_conv_in['proj_b'], 'L0_conv_skip_scale': _L0_conv_in['skip_scale'], 'L0_ffn_gate_weight': _L0_ffn_in['gate_weight'], 'L0_ffn_w1': _L0_ffn_in['w1'], 'L0_ffn_b1': _L0_ffn_in['b1'], 'L0_ffn_w2': _L0_ffn_in['w2'], 'L0_ffn_b2': _L0_ffn_in['b2']}

def reference(x, L0_conv_norm_w, L0_conv_norm_b, L0_conv_fc1_w, L0_conv_fc1_b, L0_conv_fc2_w, L0_conv_fc2_b, L0_conv_Win, L0_conv_conv_w, L0_conv_conv_b, L0_conv_Wx, L0_conv_Wdt, L0_conv_dt_bias, L0_conv_A_log, L0_conv_Dp, L0_conv_onorm_w, L0_conv_onorm_b, L0_conv_Wout, L0_conv_proj_w, L0_conv_proj_b, L0_conv_skip_scale, L0_ffn_gate_weight, L0_ffn_w1, L0_ffn_b1, L0_ffn_w2, L0_ffn_b2):
    import jax
    import jax.numpy as jnp

    def _L0_conv_ref(x, norm_w, norm_b, fc1_w, fc1_b, fc2_w, fc2_b, Win, conv_w, conv_b, Wx, Wdt, dt_bias, A_log, Dp, onorm_w, onorm_b, Wout, proj_w, proj_b, skip_scale):
        import jax, jax.numpy as jnp
        import numpy as np
        LN_EPS = 1e-05

        def layernorm(x, w, b, eps=LN_EPS):
            m = jnp.mean(x, -1, keepdims=True)
            v = jnp.mean(jnp.square(x - m), -1, keepdims=True)
            return (x - m) * jax.lax.rsqrt(v + eps) * w + b

        def to_seq(x, k):
            B, d, H, W = x.shape
            if k >= 2:
                x = jnp.swapaxes(x, 2, 3)
            s = x.reshape(B, d, H * W)
            if k % 2 == 1:
                s = s[:, :, ::-1]
            return s

        def from_seq(y, k, H, W):
            B, d, L = y.shape
            if k % 2 == 1:
                y = y[:, :, ::-1]
            if k >= 2:
                y = jnp.swapaxes(y.reshape(B, d, W, H), 2, 3)
            else:
                y = y.reshape(B, d, H, W)
            return y

        def ss2d(x, k, Win, cw, cb, Wx, Wdt, dtb, A_log, Dp, nw, nb, Wout):
            B, H, W, d = x.shape
            xz = x @ Win
            xin, z = jnp.split(xz, 2, axis=-1)
            xc = jnp.transpose(xin, (0, 3, 1, 2))
            xc = jax.lax.conv_general_dilated(xc, cw, (1, 1), ((1, 1), (1, 1)), feature_group_count=d) + cb[None, :, None, None]
            xc = jax.nn.silu(xc)
            u = to_seq(xc, k)
            x_dbl = jnp.einsum('bdl,rd->brl', u, Wx)
            dtr = Wdt.shape[1]
            N = A_log.shape[1]
            dt, Bm, Cm = jnp.split(x_dbl, [dtr, dtr + N], axis=1)
            delta = jax.nn.softplus(jnp.einsum('brl,dr->bdl', dt, Wdt) + dtb[None, :, None])
            A = -jnp.exp(A_log)
            dA = jnp.exp(delta[..., None] * A[None, :, None, :])
            dBu = (delta * u)[..., None] * jnp.transpose(Bm, (0, 2, 1))[:, None]

            def comb(c1, c2):
                a1, b1 = c1
                a2, b2 = c2
                return (a1 * a2, a2 * b1 + b2)
            _, h = jax.lax.associative_scan(comb, (dA, dBu), axis=2)
            y = jnp.einsum('bdln,bnl->bdl', h, Cm) + Dp[:, None] * u
            y = jnp.transpose(from_seq(y, k, H, W), (0, 2, 3, 1))
            y = layernorm(y, nw, nb)
            y = y * jax.nn.silu(z)
            return y @ Wout
        B, C, H, W = x.shape
        xs = jnp.transpose(x.reshape(B, C, H * W), (0, 2, 1))
        xs = layernorm(xs, norm_w, norm_b)
        z = jnp.mean(xs, axis=1)
        se = jax.nn.sigmoid(jax.nn.relu(z @ fc1_w + fc1_b) @ fc2_w + fc2_b)
        xh = xs.reshape(B, H, W, C)
        d = C // 4
        outs = [ss2d(xh[..., k * d:(k + 1) * d], k, Win[k], conv_w[k], conv_b[k], Wx[k], Wdt[k], dt_bias[k], A_log[k], Dp[k], onorm_w[k], onorm_b[k], Wout[k]) for k in range(4)]
        xm = jnp.concatenate(outs, -1) * skip_scale * xh
        xm = xm.reshape(B, H * W, C) * se[:, None, :]
        xm = layernorm(xm, norm_w, norm_b)
        xm = xm @ proj_w + proj_b
        return jnp.transpose(xm, (0, 2, 1)).reshape(B, C, H, W)

    def _L0_ffn_ref(x, gate_weight, w1, b1, w2, b2):
        import jax, jax.numpy as jnp
        import numpy as np
        B, S, D = (8, 2048, 128)
        E, DFF = (16, 128)
        CAPACITY = 2
        Bx, Sx, Dx = x.shape
        num_experts = gate_weight.shape[1]
        k = Sx // num_experts * CAPACITY
        logits = jnp.einsum('bsd,de->bse', x, gate_weight)
        affinity = jax.nn.softmax(logits, axis=-1).transpose(0, 2, 1)
        gating, index = jax.lax.top_k(affinity, k)
        x_in = jnp.take_along_axis(x[:, None, :, :], index[..., None], axis=2)
        h = jax.nn.gelu(jnp.einsum('bekd,edh->bekh', x_in, w1) + b1[None, :, None, :])
        x_e = jnp.einsum('bekh,ehd->bekd', h, w2) + b2[None, :, None, :]
        weighted = gating[..., None] * x_e
        out = jnp.zeros_like(x)
        idx_flat = index.reshape(Bx, num_experts * k)
        vals_flat = weighted.reshape(Bx, num_experts * k, Dx)
        out = out.at[jnp.arange(Bx)[:, None], idx_flat].add(vals_flat)
        return out

    def _gn(v, G=32, eps=1e-05):
        B_, C_, H_, W_ = v.shape
        g = v.reshape(B_, G, C_ // G, H_, W_)
        m = jnp.mean(g, axis=(2, 3, 4), keepdims=True)
        s = jnp.var(g, axis=(2, 3, 4), keepdims=True)
        return ((g - m) / jnp.sqrt(s + eps)).reshape(v.shape)

    def _ln_c(v, eps=1e-06):
        m = jnp.mean(v, axis=1, keepdims=True)
        s = jnp.var(v, axis=1, keepdims=True)
        return (v - m) / jnp.sqrt(s + eps)

    def _ln_t(v, eps=1e-05):
        m = jnp.mean(v, axis=-1, keepdims=True)
        s = jnp.var(v, axis=-1, keepdims=True)
        return (v - m) / jnp.sqrt(s + eps)

    def _to_tokens(v):
        B_, C_, H_, W_ = v.shape
        return v.reshape(B_, C_, H_ * W_).transpose(0, 2, 1)

    def _from_tokens(t, like):
        B_, C_, H_, W_ = like.shape
        return t.transpose(0, 2, 1).reshape(B_, C_, H_, W_)
    x = x + _L0_conv_ref(_ln_c(x), L0_conv_norm_w, L0_conv_norm_b, L0_conv_fc1_w, L0_conv_fc1_b, L0_conv_fc2_w, L0_conv_fc2_b, L0_conv_Win, L0_conv_conv_w, L0_conv_conv_b, L0_conv_Wx, L0_conv_Wdt, L0_conv_dt_bias, L0_conv_A_log, L0_conv_Dp, L0_conv_onorm_w, L0_conv_onorm_b, L0_conv_Wout, L0_conv_proj_w, L0_conv_proj_b, L0_conv_skip_scale)
    t = _to_tokens(x)
    t = t + _L0_ffn_ref(_ln_t(t), L0_ffn_gate_weight, L0_ffn_w1, L0_ffn_b1, L0_ffn_w2, L0_ffn_b2)
    x = _from_tokens(t, x)
    return x

_drawn_inputs = setup_inputs


def setup_inputs(seed=0):
    import zlib

    import numpy as np

    out = dict(_drawn_inputs(seed))
    spreads = {'L0_conv_norm_w': (1.0, 0.2),
     'L0_conv_norm_b': (0.0, 0.1),
     'L0_conv_fc1_b': (0.0, 0.8),
     'L0_conv_fc2_b': (0.0, 0.8),
     'L0_conv_conv_b': (0.0, 0.1),
     'L0_conv_dt_bias': (-4.599999904632568, 0.6),
     'L0_conv_A_log': (0.0, 2.0),
     'L0_conv_Dp': (1.0, 0.2),
     'L0_conv_onorm_w': (1.0, 0.2),
     'L0_conv_onorm_b': (0.0, 0.393),
     'L0_conv_proj_b': (0.0, 0.1),
     'L0_ffn_b1': (0.0, 0.8),
     'L0_ffn_b2': (0.0, 0.8)}
    factors = {'L0_conv_fc1_w': 8.0,
     'L0_conv_fc2_w': 8.0,
     'L0_conv_Wx': 64.0,
     'L0_conv_Wdt': 64.0,
     'L0_ffn_gate_weight': 5.994,
     'L0_ffn_w1': 8.0,
     'L0_ffn_w2': 8.0}
    for name, (base, spread) in spreads.items():
        noise = np.random.default_rng([zlib.crc32(name.encode()), seed]).standard_normal(out[name].shape)
        drawn = base * np.exp(spread * noise) if base else spread * noise
        out[name] = jnp.asarray(drawn.astype(out[name].dtype))
    for name, factor in factors.items():
        out[name] = (out[name] * factor).astype(out[name].dtype)
    return out
```

```python
from contextlib import ExitStack

import concourse.bass as bass
from concourse import mybir

ALU = mybir.AluOpType
ACT = mybir.ActivationFunctionType
AX_X = mybir.AxisListType.X
F32 = mybir.dt.float32
F32R = mybir.dt.float32r
U32 = mybir.dt.uint32

B, C, HH, WW = 16, 128, 48, 48
L = HH * WW
KD = 4
DC = C // KD
E, DFF = 16, 128
CAP = L // E * 2
R1 = C // 16
TH = 3
TL = L // TH
CH = TL // 2
CR = CH // WW
PW = WW + 2
PL = (HH + 2) * PW
SL = HH * PW
NT = L // 128
TT = TL // 128
BG = 128 // E
SOFTPLUS_MAX = 40.0

MATS = ["J128", "CEN128", "CEN32", "J32", "IDENT", "WZ", "WXT", "WDTT", "WB", "WCC", "WOUT", "PROJ", "FC2"]
VECS = ["norm_w", "norm_b", "conv_b", "dt_bias", "A_log", "Dp", "onorm_w", "onorm_b", "proj_b", "fc1_b", "fc2_b",
        "skip", "eps_in", "eps_ln"]


def build_program(nc, x, mats, vecs, fc1, gate, winx, convw, w1, b1, w2, b2, out):
    x2_dram = nc.dram_tensor("x2_dram", (B, C, L), F32).ap()
    xf_dram = nc.dram_tensor("xf_dram", (B, C, L), F32).ap()
    aff_dram = nc.dram_tensor("aff_dram", (B, E, L), F32).ap()
    gates_dram = nc.dram_tensor("gates_dram", (B, E, L), F32).ap()
    with ExitStack() as keep:
        def sb(name, shape, dt=F32):
            return keep.enter_context(nc.sbuf_tensor(name, shape, dt))

        psum = keep.enter_context(nc.psum_tensor("psum", [128, 8, 512], F32))
        mixer_phase(nc, psum, x, mats, vecs, fc1, gate, winx, convw, x2_dram, xf_dram, aff_dram)
        w1p = [sb(f"w1p{i}", [128, E, DFF], F32R) for i in range(2)]
        w2p = [sb(f"w2p{i}", [128, E, C], F32R) for i in range(2)]
        b1s = sb("b1s", [128, E])
        b2s = sb("b2s", [E, C])
        route_phase(nc, aff_dram, gates_dram, [(w1, w1p), (w2, w2p)], [(b1s, b1), (b2s, b2)])
        expert_phase(nc, psum, w1p, w2p, b1s, b2s, x2_dram, xf_dram, gates_dram, out)


def wait(eng, semaphore, value):
    if not isinstance(value, int) or value > 0:
        eng.wait_ge(semaphore, value)


def slot(psum, s):
    return psum[:, 2 * s:2 * s + 2, 0:CH]


def third(t):
    return slice(t * TL, (t + 1) * TL)


def halves(ap):
    return ap.rearrange("p (a n) -> p a n", a=2)


def done(b, t=TH - 1):
    return b * TH + (t + 1)


def in_order(k, image, c):
    if k % 2:
        image = image[:, ::-1, ::-1]
    if k >= 2:
        image = image.rearrange("p h w -> p w h")
    return image[:, c * CR:(c + 1) * CR, :]


def mixer_phase(nc, psum, x, mats, vecs, fc1, gate, winx, convw, x2_dram, xf_dram, aff_dram):
    with ExitStack() as ctx:
        def sb(name, shape):
            return ctx.enter_context(nc.sbuf_tensor(name, shape, F32))

        def sem(name):
            return ctx.enter_context(nc.semaphore(name))

        ident = sb("ident", [128, 128])
        m_all = sb("m_all", [128, len(MATS), 128])
        M = {n: m_all[:, i, :] for i, n in enumerate(MATS)}
        v_all = sb("v_all", [128, len(VECS)])
        V = {n: v_all[:, i:i + 1] for i, n in enumerate(VECS)}
        fc1s = sb("fc1s", [128, R1])
        gates = sb("gates", [128, E])
        winxs = sb("winxs", [96, KD, DC])
        convws = sb("convws", [96, KD, 3, DC])
        wconv = sb("wconv", [96, KD, 3, DC])
        wdelta = sb("wdelta", [128, 128])
        dpcen = sb("dpcen", [128, 128])
        projw = sb("projw", [128, 128])
        projc = sb("projc", [128, 128])
        vx = sb("vx", [128, 4])
        a_neg, fc2_neg, proj_c, a_exp = (vx[:, i:i + 1] for i in range(4))

        X = [sb(f"X{i}", [128, L]) for i in range(2)]
        XS = [sb(f"XS{i}", [128, PL]) for i in range(2)]
        zsum = [sb(f"zsum{i}", [128, TH]) for i in range(2)]
        stack = sb("stack", [96, KD, SL])
        SQ = sb("SQ", [128, L])
        RS = sb("RS", [128, L])
        U = sb("U", [128, L])
        ZS = sb("ZS", [128, L])
        CLXM = sb("CLXM", [128, L])
        DH = sb("DH", [128, L])
        DA = sb("DA", [128, L])
        DU = sb("DU", [128, L])
        G = sb("G", [128, L])
        X2 = sb("X2", [128, L])
        XF = sb("XF", [128, L])
        se1 = sb("se1", [R1, 1])
        sex = sb("sex", [128, 1])
        s1 = sb("s1", [128, 3])
        lg = sb("lg", [128, NT, E])
        aff = sb("aff", [128, NT, E])
        lgst = sb("lgst", [128, 3, NT])

        names = ("consts border_zero prep_exp prep_vec prep_mm prep_done x_loaded stacked x2_stored xf_stored aff_stored "
                 "cen1_pe sq1 var1_pe ln1 rstd1 xn xs "
                 "conv_pe u z_pe zs fc1_pe relu1 fc2_pe sex_exp se_add se_done "
                 "pre_pe clamped sp_exp sp_ln delta du_pool decay bc_pe dbu cc_pe h hc "
                 "yc_pe sq2 var2_pe ln2 rstd2 yn g "
                 "out_pe xm cen3_pe sq3 var3_pe ln3 rstd3 proj_pe pr x2 "
                 "cen4_pe sq4 var4_pe ln4 rstd4 xf "
                 "lg_pe lg_max lg_sub lg_exp lg_sum lg_rec aff_ready afft_pe afft").split()
        S = {n: sem("m_" + n) for n in names}

        def run(eng, front, mid, tail):
            def pair(b0, ends=False):
                for par in range(2):
                    b = b0 + par
                    last = ends and par == 1
                    mid(b, par)
                    if not last:
                        front(b + 1, 1 - par)
                    tail(b, par, last)

            front(0, 0)
            pair(0)
            with eng.Fori(1, B // 2 - 1) as i:
                pair(i * 2)
            pair(B - 2, ends=True)

        block = ctx.enter_context(nc.Block())

        @block.sync
        def _(sp):
            for dst, src in ((m_all[:], mats), (v_all[:], vecs), (fc1s[:], fc1), (gates[:], gate),
                             (winxs[:], winx), (convws[:], convw), (ident[:], mats[:, MATS.index("IDENT"), :])):
                sp.dma_start(dst, src).then_inc(S["consts"], 16)

            def load(b, par):
                sp.dma_start(X[par][:], x[b]).then_inc(S["x_loaded"], 16)

            def front(b, par):
                wait(sp, S["xs"], done(b))
                wait(sp, S["conv_pe"], b * TH)
                for j in range(3):
                    for k in range(KD):
                        sp.dma_start(stack[DC * j:DC * j + DC, k, :],
                                     XS[par][DC * k:DC * k + DC, j * PW:j * PW + SL]).then_inc(S["stacked"], 16)

            def mid(b, par):
                if isinstance(b, int) and b == B - 1:
                    return
                wait(sp, S["x2"], b * TH)
                load(b + 1, 1 - par)

            def tail(b, par, last):
                wait(sp, S["x2"], done(b))
                sp.dma_start(x2_dram[b], X2[:]).then_inc(S["x2_stored"], 16)
                wait(sp, S["xf"], done(b))
                sp.dma_start(xf_dram[b], XF[:]).then_inc(S["xf_stored"], 16)
                wait(sp, S["afft"], done(b))
                sp.dma_start(aff_dram[b], DA[0:E, :]).then_inc(S["aff_stored"], 16)

            load(0, 0)
            run(sp, front, mid, tail)
            for s in ("x2_stored", "xf_stored", "aff_stored"):
                wait(sp, S[s], 16 * B)

        @block.gpsimd
        def _(pool):
            for i in range(2):
                nc.gpsimd.memset(XS[i][:], 0.0).then_inc(S["border_zero"], 1)

            def front(b, par):
                pass

            def mid(b, par):
                wait(pool, S["yc_pe"], b * TH)
                for t in range(TH):
                    wait(pool, S["delta"], done(b, t))
                    wait(pool, S["u"], done(b, t))
                    nc.gpsimd.tensor_tensor(DU[:, third(t)], DH[:, third(t)], U[:, third(t)],
                                            ALU.mult).then_inc(S["du_pool"], 1)

            def tail(b, par, last):
                pass

            run(pool, front, mid, tail)

        @block.scalar
        def _(act):
            def rstd(ln, ps, b, t, out_sem, eps, scale=1.0):
                nc.scalar.activation(halves(RS[:, third(t)]), slot(psum, ps), ACT.Ln, bias=V[eps],
                                     scale=scale).then_inc(S[ln], 1)
                wait(act, S[ln], done(b, t))
                nc.scalar.activation(RS[:, third(t)], RS[:, third(t)], ACT.Exp, scale=-0.5).then_inc(S[out_sem], 1)

            act.preload_act_table_set("natural_log_exp_and_others")
            wait(act, S["consts"], 16 * 7)
            nc.scalar.activation(a_exp, V["A_log"], ACT.Exp).then_inc(S["prep_exp"], 1)
            wait(act, S["prep_done"], 3)
            wait(act, S["border_zero"], 2)

            def front(b, par):
                first = isinstance(b, int) and b == 0
                for t in range(TH):
                    wait(act, S["cen1_pe"], done(b, t))
                    if not first:
                        wait(act, S["var2_pe"], done(b - 1, t))
                    nc.scalar.activation(halves(SQ[:, third(t)]), slot(psum, t), ACT.Square).then_inc(S["sq1"], 1)
                for t in range(TH):
                    wait(act, S["var1_pe"], done(b, t))
                    if not first:
                        wait(act, S["yn"], done(b - 1, t))
                    rstd("ln1", 3, b, t, "rstd1", "eps_in", 1.0 + 1e-5)
                for t in range(TH):
                    wait(act, S["xn"], done(b, t))
                    view = XS[par][:].rearrange("p (h w) -> p h w", w=PW)[:, 1 + 16 * t:17 + 16 * t, 1:1 + WW]
                    nc.scalar.activation(view, view, ACT.Identity, bias=V["norm_b"],
                                         accum_out=zsum[par][:, t:t + 1]).then_inc(S["xs"], 1)

            def mid(b, par):
                wait(act, S["yc_pe"], b * TH)
                for t in range(TH):
                    wait(act, S["conv_pe"], done(b, t))
                    nc.scalar.activation(halves(U[:, third(t)]), slot(psum, t), ACT.Silu,
                                         bias=V["conv_b"]).then_inc(S["u"], 1)
                wait(act, S["g"], b * TH)
                for t in range(TH):
                    wait(act, S["z_pe"], done(b, t))
                    nc.scalar.activation(halves(ZS[:, third(t)]), slot(psum, (3, 0, 1)[t]),
                                         ACT.Silu).then_inc(S["zs"], 1)
                act.preload_act_table_set("natural_log_exp_and_others")
                wait(act, S["fc1_pe"], b + 1)
                nc.scalar.activation(se1[:], psum[0:R1, 4, 0:1], ACT.Relu, bias=V["fc1_b"][0:R1],
                                     scale=1.0 / L).then_inc(S["relu1"], 1)
                wait(act, S["fc2_pe"], b + 1)
                nc.scalar.activation(sex[:], psum[:, 4, 0:1], ACT.Exp, bias=fc2_neg, scale=-1.0).then_inc(S["sex_exp"], 1)
                for t in range(TH):
                    wait(act, S["clamped"], done(b, t))
                    nc.scalar.activation(CLXM[:, third(t)], CLXM[:, third(t)], ACT.Exp).then_inc(S["sp_exp"], 1)
                    wait(act, S["sp_exp"], done(b, t))
                    nc.scalar.activation(CLXM[:, third(t)], CLXM[:, third(t)], ACT.Ln, bias=1.0).then_inc(S["sp_ln"], 1)
                wait(act, S["h"], b * TH)
                wait(act, S["aff_stored"], b * 16)
                for t in range(TH):
                    wait(act, S["delta"], done(b, t))
                    nc.scalar.activation(DA[:, third(t)], DH[:, third(t)], ACT.Exp, scale=a_neg).then_inc(S["decay"], 1)
                wait(act, S["var4_pe"], b * TH)
                for t in range(TH):
                    wait(act, S["yc_pe"], done(b, t))
                    nc.scalar.activation(halves(SQ[:, third(t)]), slot(psum, t), ACT.Square).then_inc(S["sq2"], 1)
                wait(act, S["xf"], b * TH)
                for t in range(TH):
                    wait(act, S["var2_pe"], done(b, t))
                    rstd("ln2", 3, b, t, "rstd2", "eps_ln")

            def tail(b, par, last):
                for t in range(TH):
                    wait(act, S["cen3_pe"], done(b, t))
                    wait(act, *((S["var2_pe"], done(b, t)) if last else (S["var1_pe"], done(b + 1, t))))
                    nc.scalar.activation(halves(SQ[:, third(t)]), slot(psum, (3, 0, 1)[t]),
                                         ACT.Square).then_inc(S["sq3"], 1)
                for t in range(TH):
                    wait(act, S["var3_pe"], done(b, t))
                    wait(act, *((S["yn"], done(b, t)) if last else (S["xn"], done(b + 1, t))))
                    rstd("ln3", (2, 3, 0)[t], b, t, "rstd3", "eps_ln")
                for t in range(TH):
                    wait(act, S["cen4_pe"], done(b, t))
                    wait(act, S["var3_pe"], done(b, t))
                    nc.scalar.activation(halves(SQ[:, third(t)]), slot(psum, t), ACT.Square).then_inc(S["sq4"], 1)
                for t in range(TH):
                    wait(act, S["var4_pe"], done(b, t))
                    wait(act, S["pr"], done(b, t))
                    rstd("ln4", 3, b, t, "rstd4", "eps_ln")
                wait(act, S["lg_sub"], b + 1)
                nc.scalar.activation(lg[:], lg[:], ACT.Exp).then_inc(S["lg_exp"], 1)
                wait(act, S["h"], done(b))
                for t in range(TH):
                    wait(act, S["afft_pe"], done(b, t))
                    nc.scalar.activation(halves(DA[0:E, third(t)]), psum[0:E, 2 + 2 * t:4 + 2 * t, 0:CH],
                                         ACT.Copy).then_inc(S["afft"], 1)

            run(act, front, mid, tail)

        @block.vector
        def _(dve):
            v = nc.vector
            wait(dve, S["consts"], 16 * 7)
            for dx in range(3):
                v.tensor_tensor(wconv[:, :, dx, :], winxs[:], convws[:, :, dx, :], ALU.mult).then_inc(S["prep_vec"], 1)
            v.tensor_scalar(dpcen[:], M["CEN32"], V["Dp"], None, ALU.mult).then_inc(S["prep_vec"], 1)
            v.tensor_scalar(projw[:], M["PROJ"], V["norm_w"], None, ALU.mult).then_inc(S["prep_vec"], 1)
            v.tensor_scalar(fc2_neg, V["fc2_b"], -1.0, None, ALU.mult).then_inc(S["prep_vec"], 1)
            wait(dve, S["prep_exp"], 1)
            v.tensor_scalar(a_neg, a_exp, -1.0, None, ALU.mult).then_inc(S["prep_vec"], 1)
            wait(dve, S["prep_mm"], 3)
            v.tensor_copy(wdelta[:], psum[:, 0, 0:128]).then_inc(S["prep_done"], 1)
            v.tensor_copy(projc[:], psum[:, 2, 0:128]).then_inc(S["prep_done"], 1)
            v.tensor_tensor(proj_c, psum[:, 4, 0:1], V["proj_b"], ALU.add).then_inc(S["prep_done"], 1)
            wait(dve, S["prep_vec"], 7)
            wait(dve, S["prep_done"], 3)
            wait(dve, S["border_zero"], 2)

            def interior(par, t):
                return XS[par][:].rearrange("p (h w) -> p h w", w=PW)[:, 1 + 16 * t:17 + 16 * t, 1:1 + WW]

            def rows(ap):
                return ap.rearrange("p (a h w) -> p a h w", a=2, w=WW)

            def ps_rows(s):
                return slot(psum, s).rearrange("p a (h w) -> p a h w", w=WW)

            def front(b, par):
                for t in range(TH):
                    wait(dve, S["rstd1"], done(b, t))
                    v.scalar_tensor_tensor(interior(par, t).rearrange("p (a h) w -> p a h w", a=2), ps_rows(t),
                                           V["norm_w"], rows(RS[:, third(t)]), ALU.mult, ALU.mult).then_inc(S["xn"], 1)

            def mid(b, par):
                wait(dve, S["proj_pe"], b * TH)
                for t in range(TH):
                    wait(dve, S["pre_pe"], done(b, t))
                    v.tensor_scalar(halves(CLXM[:, third(t)]), slot(psum, (3, 0, 1)[t]), V["dt_bias"], SOFTPLUS_MAX,
                                    ALU.add, ALU.min).then_inc(S["clamped"], 1)
                wait(dve, S["sex_exp"], b + 1)
                wait(dve, S["xm"], b * TH)
                v.tensor_scalar(s1[:, 0:1], sex[:], 1.0, None, ALU.add).then_inc(S["se_add"], 1)
                wait(dve, S["se_add"], b * 2 + 1)
                v.reciprocal(s1[:, 1:2], s1[:, 0:1]).then_inc(S["se_add"], 1)
                wait(dve, S["se_add"], b * 2 + 2)
                v.tensor_tensor(s1[:, 2:3], s1[:, 1:2], V["skip"], ALU.mult).then_inc(S["se_done"], 1)
                wait(dve, S["yc_pe"], b * TH)
                for t in range(TH):
                    wait(dve, S["sp_ln"], done(b, t))
                    v.scalar_tensor_tensor(halves(DH[:, third(t)]), slot(psum, (3, 0, 1)[t]), V["dt_bias"],
                                           halves(CLXM[:, third(t)]), ALU.add, ALU.max).then_inc(S["delta"], 1)

                def dbu(t):
                    wait(dve, S["bc_pe"], done(b, t))
                    wait(dve, S["du_pool"], done(b, t))
                    v.tensor_tensor(halves(DU[:, third(t)]), halves(DU[:, third(t)]), slot(psum, (2, 3, 0)[t]),
                                    ALU.mult).then_inc(S["dbu"], 1)

                def scan(t):
                    wait(dve, S["decay"], done(b, t))
                    wait(dve, S["dbu"], done(b, t))
                    if t:
                        wait(dve, S["h"], done(b, t - 1))
                    v.tensor_tensor_scan(DH[:, third(t)], DA[:, third(t)], DU[:, third(t)],
                                         DH[:, t * TL - 1:t * TL] if t else 0.0, ALU.mult, ALU.add).then_inc(S["h"], 1)

                def hc(t):
                    wait(dve, S["cc_pe"], done(b, t))
                    wait(dve, S["h"], done(b, t))
                    v.tensor_tensor(halves(DU[:, third(t)]), halves(DH[:, third(t)]), slot(psum, (1, 2, 3)[t]),
                                    ALU.mult).then_inc(S["hc"], 1)

                dbu(0)
                scan(0)
                dbu(1)
                hc(0)
                scan(1)
                dbu(2)
                hc(1)
                scan(2)
                hc(2)
                wait(dve, S["out_pe"], b * TH)
                for t in range(TH):
                    wait(dve, S["rstd2"], done(b, t))
                    v.scalar_tensor_tensor(halves(G[:, third(t)]), slot(psum, t), V["onorm_w"], halves(RS[:, third(t)]),
                                           ALU.mult, ALU.mult).then_inc(S["yn"], 1)
                    wait(dve, S["yn"], done(b, t))
                    wait(dve, S["zs"], done(b, t))
                    v.scalar_tensor_tensor(G[:, third(t)], G[:, third(t)], V["onorm_b"], ZS[:, third(t)],
                                           ALU.add, ALU.mult).then_inc(S["g"], 1)

            def tail(b, par, last):
                wait(dve, S["se_done"], b + 1)
                for t in range(TH):
                    wait(dve, S["out_pe"], done(b, t))
                    v.scalar_tensor_tensor(rows(CLXM[:, third(t)]), interior(par, t).rearrange("p (a h) w -> p a h w", a=2),
                                           s1[:, 2:3], ps_rows(t), ALU.mult, ALU.mult).then_inc(S["xm"], 1)
                wait(dve, S["x2_stored"], b * 16)
                wait(dve, S["cen4_pe"], b * TH)
                for t in range(TH):
                    wait(dve, S["proj_pe"], done(b, t))
                    wait(dve, S["rstd3"], done(b, t))
                    v.tensor_tensor(halves(X2[:, third(t)]), slot(psum, (1, 2, 3)[t]), halves(RS[:, third(t)]),
                                    ALU.mult).then_inc(S["pr"], 1)
                    wait(dve, S["pr"], done(b, t))
                    v.scalar_tensor_tensor(X2[:, third(t)], X2[:, third(t)], proj_c, X[par][:, third(t)],
                                           ALU.add, ALU.add).then_inc(S["x2"], 1)
                wait(dve, S["xf_stored"], b * 16)
                wait(dve, S["lg_pe"], b)
                for t in range(TH):
                    wait(dve, S["rstd4"], done(b, t))
                    v.tensor_tensor(halves(XF[:, third(t)]), slot(psum, t), halves(RS[:, third(t)]),
                                    ALU.mult).then_inc(S["xf"], 1)
                wait(dve, S["lg_pe"], b + 1)
                lp = psum[:, 0, 0:NT * E].rearrange("p (t e) -> p t e", e=E)
                v.tensor_reduce(lgst[:, 0, :], lp, AX_X, ALU.max).then_inc(S["lg_max"], 1)
                wait(dve, S["lg_max"], b + 1)
                v.tensor_tensor(lg[:], lp, lgst[:, 0, :].unsqueeze(2).to_broadcast([128, NT, E]),
                                ALU.subtract).then_inc(S["lg_sub"], 1)
                wait(dve, S["lg_exp"], b + 1)
                v.tensor_reduce(lgst[:, 1, :], lg[:], AX_X, ALU.add).then_inc(S["lg_sum"], 1)
                wait(dve, S["lg_sum"], b + 1)
                v.reciprocal(lgst[:, 2, :], lgst[:, 1, :]).then_inc(S["lg_rec"], 1)
                wait(dve, S["lg_rec"], b + 1)
                wait(dve, S["afft_pe"], b * TH)
                v.tensor_tensor(aff[:], lg[:], lgst[:, 2, :].unsqueeze(2).to_broadcast([128, NT, E]),
                                ALU.mult).then_inc(S["aff_ready"], 1)

            run(dve, front, mid, tail)

        @block.tensor
        def _(pe):
            mm = nc.tensor.matmul

            def full(s, w, src, t):
                for a in range(2):
                    last = mm(psum[:, 2 * s + a, 0:CH], w, src[:, t * TL + a * CH:t * TL + (a + 1) * CH],
                              start=True, stop=True)
                return last

            wait(pe, S["consts"], 16 * 7)
            wait(pe, S["prep_vec"], 7)
            mm(psum[:, 0, 0:128], M["WXT"][0:32], M["WDTT"][0:32], start=True, stop=True).then_inc(S["prep_mm"], 1)
            mm(psum[:, 2, 0:128], M["CEN128"], projw[:], start=True, stop=True).then_inc(S["prep_mm"], 1)
            mm(psum[:, 4, 0:1], M["PROJ"], V["norm_b"], start=True, stop=True).then_inc(S["prep_mm"], 1)
            wait(pe, S["prep_done"], 3)

            def front(b, par):
                first = isinstance(b, int) and b == 0
                wait(pe, S["x_loaded"], b * 16 + 16)
                for t in range(TH):
                    if not first:
                        wait(pe, S["yn"], done(b - 1, t))
                    full(t, M["CEN128"], X[par], t).then_inc(S["cen1_pe"], 1)
                for t in range(TH):
                    wait(pe, S["sq1"], done(b, t))
                    if t:
                        wait(pe, S["ln1"], done(b, t - 1))
                    elif not first:
                        wait(pe, S["ln2"], done(b - 1))
                    full(3, M["J128"], SQ, t).then_inc(S["var1_pe"], 1)

            def mid(b, par):
                wait(pe, S["stacked"], (b + 1) * (3 * KD * 16))
                for t in range(TH):
                    if t == 0:
                        wait(pe, S["lg_sub"], b)
                    else:
                        wait(pe, S["afft"], b * TH)
                    for a in range(2):
                        for dx in range(3):
                            for k in range(KD):
                                img = stack[:, k, :].rearrange("p (h w) -> p h w", w=PW)[:, :, dx:dx + WW]
                                last = mm(psum[32 * k:32 * k + 32, 2 * t + a, 0:CH], wconv[:, k, dx, :],
                                          in_order(k, img, 2 * t + a), start=(dx == 0), stop=(dx == 2))
                    last.then_inc(S["conv_pe"], 1)
                for t in range(TH):
                    s = (3, 0, 1)[t]
                    if t:
                        wait(pe, S["u"], done(b, t - 1))
                    for a in range(2):
                        for k in range(KD):
                            img = XS[par][:].rearrange("p (h w) -> p h w", w=PW)[:, 1:1 + HH, 1:1 + WW]
                            last = mm(psum[32 * k:32 * k + 32, 2 * s + a, 0:CH], M["WZ"][:, 32 * k:32 * k + 32],
                                      in_order(k, img, 2 * t + a), start=True, stop=True)
                    last.then_inc(S["z_pe"], 1)
                wait(pe, S["u"], done(b))
                for t in range(TH):
                    last = mm(psum[0:R1, 4, 0:1], fc1s[:], zsum[par][:, t:t + 1], start=(t == 0), stop=(t == TH - 1))
                last.then_inc(S["fc1_pe"], 1)
                for t in range(TH):
                    wait(pe, S["zs"], done(b, t))
                    full((3, 0, 1)[t], wdelta[:], U, t).then_inc(S["pre_pe"], 1)
                wait(pe, S["relu1"], b + 1)
                mm(psum[:, 4, 0:1], M["FC2"][0:R1], se1[:], start=True, stop=True).then_inc(S["fc2_pe"], 1)
                for t in range(TH):
                    if t == 0:
                        wait(pe, S["sex_exp"], b + 1)
                    else:
                        wait(pe, S["delta"], done(b, t - 1))
                    full((2, 3, 0)[t], M["WB"], U, t).then_inc(S["bc_pe"], 1)
                for t in range(TH):
                    if t == 0:
                        wait(pe, S["delta"], done(b, 2))
                    else:
                        wait(pe, S["dbu"], done(b, t - 1))
                    full((1, 2, 3)[t], M["WCC"], U, t).then_inc(S["cc_pe"], 1)
                for t in range(TH):
                    wait(pe, S["dbu"], done(b))
                    wait(pe, S["hc"], done(b, t))
                    for a in range(2):
                        cols = slice(t * TL + a * CH, t * TL + (a + 1) * CH)
                        mm(psum[:, 2 * t + a, 0:CH], M["CEN32"], DU[:, cols], start=True, stop=False)
                        last = mm(psum[:, 2 * t + a, 0:CH], dpcen[:], U[:, cols], start=False, stop=True)
                    last.then_inc(S["yc_pe"], 1)
                for t in range(TH):
                    wait(pe, S["sq2"], done(b, t))
                    if t:
                        wait(pe, S["ln2"], done(b, t - 1))
                    full(3, M["J32"], SQ, t).then_inc(S["var2_pe"], 1)

            def tail(b, par, last_image):
                wait(pe, S["g"], done(b))
                for t in range(TH):
                    wait(pe, *((S["yn"], done(b, t)) if last_image else (S["xn"], done(b + 1, t))))
                    for a in range(2):
                        for k in range(KD):
                            seq = G[:].rearrange("p (h w) -> p h w", w=WW)
                            last = mm(psum[32 * k:32 * k + 32, 2 * t + a, 0:CH], M["WOUT"][:, 32 * k:32 * k + 32],
                                      in_order(k, seq, 2 * t + a), start=True, stop=True)
                    last.then_inc(S["out_pe"], 1)
                for t in range(TH):
                    if t == 0:
                        wait(pe, *((S["ln2"], done(b)) if last_image else (S["ln1"], done(b + 1))))
                    wait(pe, S["xm"], done(b, t))
                    full((3, 0, 1)[t], M["CEN128"], CLXM, t).then_inc(S["cen3_pe"], 1)
                wait(pe, S["xm"], done(b))
                for t in range(TH):
                    wait(pe, S["sq3"], done(b, t))
                    full((2, 3, 0)[t], M["J128"], SQ, t).then_inc(S["var3_pe"], 1)
                for t in range(TH):
                    if t:
                        wait(pe, S["ln3"], done(b, t - 1))
                    full((1, 2, 3)[t], projc[:], CLXM, t).then_inc(S["proj_pe"], 1)
                for t in range(TH):
                    if t == 0:
                        wait(pe, S["ln3"], done(b))
                    wait(pe, S["x2"], done(b, t))
                    full(t, M["CEN128"], X2, t).then_inc(S["cen4_pe"], 1)
                wait(pe, S["pr"], done(b))
                for t in range(TH):
                    wait(pe, S["sq4"], done(b, t))
                    if t:
                        wait(pe, S["ln4"], done(b, t - 1))
                    full(3, M["J128"], SQ, t).then_inc(S["var4_pe"], 1)
                wait(pe, S["xf"], done(b))
                for n in range(NT):
                    last = mm(psum[:, 0, n * E:(n + 1) * E], XF[:, n * 128:(n + 1) * 128], gates[:], start=True, stop=True)
                last.then_inc(S["lg_pe"], 1)
                wait(pe, S["aff_ready"], b + 1)
                wait(pe, S["ln4"], done(b))
                for t in range(TH):
                    for n in range(TT):
                        bank, col = 2 + 2 * t + n // 3, n % 3 * 128
                        last = nc.tensor.transpose(psum[0:E, bank, col:col + 128], aff[:, t * TT + n, :], ident[:])
                    last.then_inc(S["afft_pe"], 1)

            run(pe, front, mid, tail)


def route_phase(nc, aff_dram, gates_dram, splits, loads):
    NG = B // BG
    BITS = 30
    with ExitStack() as ctx:
        def sb(name, shape, dt=F32):
            return ctx.enter_context(nc.sbuf_tensor(name, shape, dt))

        def sem(name):
            return ctx.enter_context(nc.semaphore(name))

        A = [sb(f"A{g}", [128, L]) for g in range(NG)]
        W = [sb(f"W{g}", [128, L]) for g in range(NG)]
        Q = [sb(f"Q{g}", [128, L]) for g in range(NG)]
        whole = [sb(f"whole{n}", [128, E, 128]) for n in range(len(splits))]
        thr = [sb(f"thr{g}", [128, 1], U32) for g in range(NG)]
        cand = [sb(f"cand{g}", [128, 1], U32) for g in range(NG)]
        take = [sb(f"take{g}", [128, 1], U32) for g in range(NG)]
        cnt = [sb(f"cnt{g}", [128, 1]) for g in range(NG)]
        bit = sb("bit", [128, 1])
        bit_u = sb("bit_u", [128, 1], U32)
        w_loaded, b_loaded, a_loaded, gates_stored = (sem("r_" + n) for n in ("w_loaded", "b_loaded", "a_loaded", "gates_stored"))
        step = sem("r_step")
        gated, high_part, low_part = sem("r_gated"), sem("r_high_part"), sem("r_low_part")
        block = ctx.enter_context(nc.Block())

        @block.sync
        def _(sp):
            for g in range(NG):
                sp.dma_start(A[g][:], aff_dram[g * BG:(g + 1) * BG].rearrange("b e n -> (b e) n")).then_inc(a_loaded, 16)
            for n, (src, _) in enumerate(splits):
                sp.dma_start(whole[n][:], src).then_inc(w_loaded, 16)
            for dst, src in loads:
                sp.dma_start(dst[:], src).then_inc(b_loaded, 16)
            for g in range(NG):
                sp.wait_ge(gated, g + 1)
                sp.dma_start(gates_dram[g * BG:(g + 1) * BG].rearrange("b e n -> (b e) n"), W[g][:]).then_inc(gates_stored, 16)
            sp.wait_ge(b_loaded, 16 * len(loads))
            sp.wait_ge(gates_stored, 16 * NG)

        @block.scalar
        def _(act):
            act.wait_ge(w_loaded, 16 * len(splits))
            for n, (_, parts) in enumerate(splits):
                nc.scalar.activation(parts[0][:], whole[n][:], ACT.Copy).then_inc(high_part, 1)

        @block.gpsimd
        def _(pool):
            for n, (_, parts) in enumerate(splits):
                pool.wait_ge(high_part, n + 1)
                nc.gpsimd.tensor_tensor(parts[1][:], whole[n][:], parts[0][:].bitcast(F32),
                                        ALU.subtract).then_inc(low_part, 1)

        @block.vector
        def _(dve):
            v = nc.vector
            for g in range(NG):
                v.memset(thr[g][:], 0).then_inc(step, 1)
            v.memset(bit[:], float(2 ** (BITS - 1))).then_inc(step, 1)
            dve.wait_ge(a_loaded, 16 * NG)
            per = 2 + 4 * NG
            with dve.Fori(0, BITS) as i:
                base = i * per + (NG + 1)
                dve.wait_ge(step, base)
                v.tensor_copy(bit_u[:], bit[:]).then_inc(step, 1)
                dve.wait_ge(step, base + 1)
                for g in range(NG):
                    v.tensor_tensor(cand[g][:], thr[g][:], bit_u[:], ALU.bitwise_or).then_inc(step, 1)
                dve.wait_ge(step, base + 1 + NG)
                for g in range(NG):
                    v.tensor_scalar(Q[g][:], A[g][:], cand[g][:].bitcast(F32), 0.0, ALU.is_ge, ALU.add,
                                    accum_out=cnt[g][:]).then_inc(step, 1)
                dve.wait_ge(step, base + 1 + 2 * NG)
                for g in range(NG):
                    v.tensor_scalar(take[g][:], cnt[g][:], float(CAP), bit[:], ALU.is_ge, ALU.mult).then_inc(step, 1)
                dve.wait_ge(step, base + 1 + 3 * NG)
                for g in range(NG):
                    v.tensor_tensor(thr[g][:], thr[g][:], take[g][:], ALU.bitwise_or).then_inc(step, 1)
                v.tensor_scalar(bit[:], bit[:], 0.5, None, ALU.mult).then_inc(step, 1)
            n = BITS * per + NG + 1
            dve.wait_ge(step, n)
            for g in range(NG):
                t = thr[g][:].bitcast(F32)
                v.tensor_scalar(W[g][:], A[g][:], t, 0.0, ALU.is_gt, ALU.add, accum_out=cnt[g][:]).then_inc(step, 1)
                v.tensor_scalar(Q[g][:], A[g][:], t, None, ALU.is_equal).then_inc(step, 1)
                dve.wait_ge(step, n + 2)
                v.tensor_scalar(cnt[g][:], cnt[g][:], -1.0, float(CAP), ALU.mult, ALU.add).then_inc(step, 1)
                v.tensor_tensor_scan(W[g][:], Q[g][:], Q[g][:], 0.0, ALU.add, ALU.max).then_inc(step, 1)
                dve.wait_ge(step, n + 4)
                v.scalar_tensor_tensor(Q[g][:], W[g][:], cnt[g][:], Q[g][:], ALU.is_le, ALU.mult).then_inc(step, 1)
                dve.wait_ge(step, n + 5)
                v.scalar_tensor_tensor(Q[g][:], A[g][:], t, Q[g][:], ALU.is_gt, ALU.add).then_inc(step, 1)
                dve.wait_ge(step, n + 6)
                v.tensor_tensor(W[g][:], A[g][:], Q[g][:], ALU.mult).then_inc(gated, 1)
                n += 6


def expert_phase(nc, psum, w1p, w2p, b1s, b2s, x2_dram, xf_dram, gates_dram, out):
    UN = TH * E
    LAG_PARTS = 1
    LAG_OUT = 3
    LAG_FIN = 4
    NH, NGB = 4, 4
    with ExitStack() as ctx:
        def sb(name, shape, dt=F32):
            return ctx.enter_context(nc.sbuf_tensor(name, shape, dt))

        def sem(name):
            return ctx.enter_context(nc.semaphore(name))

        XF = [sb(f"xf{t}", [128, TL]) for t in range(TH)]
        XFP = [[sb(f"xfp{t}_{i}", [128, TL], F32R) for i in range(2)] for t in range(TH)]
        X2 = [sb(f"x2{t}", [128, TL]) for t in range(TH)]
        GR = [sb(f"gr{t}", [E, TL]) for t in range(TH)]
        GQ = [sb(f"gq{t}", [128, E // 4, TL]) for t in range(TH)]
        OUT = [sb(f"o{t}", [128, TL]) for t in range(TH)]
        Hd = [sb(f"hd{i}", [128, TL]) for i in range(NH)]
        HP = [[sb(f"hp{i}_{j}", [128, TL], F32R) for j in range(2)] for i in range(NH)]
        GB = [sb(f"gb{i}", [128, TL]) for i in range(NGB)]
        loaded, stored = [sem(f"e_loaded{t}") for t in range(TH)], [sem(f"e_stored{t}") for t in range(TH)]
        pool_turn = sem("e_pool_turn")
        xf_high, xf_split, layer1, gelu, gates_spread, gated, high, low, layer2, fin = (
            sem("e_" + n) for n in ("xf_high", "xf_split", "layer1", "gelu", "gates_spread", "gated", "high", "low", "layer2", "fin"))
        block = ctx.enter_context(nc.Block())

        def units(eng, step, lag):
            for u in range(UN):
                step(0, u, False)
            with eng.Fori(1, B) as b:
                for u in range(UN):
                    step(b, u, False)
            for u in range(lag):
                step(B, u, True)

        def behind(b, u, lag):
            if u >= lag:
                return not (isinstance(b, int) and b == B), b, u - lag
            return not (isinstance(b, int) and b == 0), b - 1, u - lag + UN

        @block.sync
        def _(sp):
            def load(b, t):
                sp.dma_start(XF[t][:], xf_dram[b, :, third(t)]).then_inc(loaded[t], 16)
                sp.dma_start(GQ[t][0:97:32, :, :],
                             gates_dram[b, :, third(t)].rearrange("(q j) n -> q j n", q=4)).then_inc(loaded[t], 16)
                sp.dma_start(GR[t][:], gates_dram[b, :, third(t)]).then_inc(loaded[t], 16)
                sp.dma_start(X2[t][:], x2_dram[b, :, third(t)]).then_inc(loaded[t], 16)

            def store(b, t):
                sp.wait_ge(fin, done(b, t))
                sp.dma_start(out[b, :, third(t)], OUT[t][:]).then_inc(stored[t], 16)

            for t in range(TH):
                load(0, t)
            with sp.Fori(1, B) as b:
                for t in range(TH):
                    store(b - 1, t)
                    load(b, t)
            for t in range(TH):
                store(B - 1, t)
            for t in range(TH):
                sp.wait_ge(stored[t], 16 * B)

        @block.gpsimd
        def _(pool):
            def step(b, u, late):
                t, e = divmod(u, E)
                if e == 0:
                    pool.wait_ge(loaded[t], (b + 1) * 64)
                    wait(pool, gates_spread, b * UN + u)
                    pool.sem_inc(pool_turn, 1)
                    nc.gpsimd.tensor_copy(XFP[t][0][:], XF[t][:]).then_inc(xf_high, 1)
                    pool.wait_ge(xf_high, done(b, t))
                    nc.gpsimd.tensor_tensor(XFP[t][1][:], XF[t][:], XFP[t][0][:].bitcast(F32),
                                            ALU.subtract).then_inc(xf_split, 1)
                    pool.wait_ge(xf_split, done(b, t))
                wait(pool, gated, b * UN + (u - NGB + 1))
                pool.sem_inc(pool_turn, 1)
                q, j = divmod(e, 4)
                nc.gpsimd.partition_broadcast(GB[u % NGB][:], GQ[t][32 * q:32 * q + 1, j, :]).then_inc(gates_spread, 1)

            units(pool, step, 0)

        @block.tensor
        def _(pe):
            def product(s, weights, parts, before=False, **flags):
                passes = [(0, 0), (0, 1), (1, 0)]
                for n, (i, j) in enumerate(passes):
                    for a in range(2):
                        last = nc.tensor.matmul(psum[:, 2 * s + a, 0:CH], weights[i], parts[j][:, a * CH:(a + 1) * CH],
                                                start=(n == 0 and not before), stop=(n == 2 and flags.get("close", True)))
                return last

            def step(b, u, late):
                if not late:
                    t, e = divmod(u, E)
                    if e == 0:
                        pe.wait_ge(xf_split, done(b, t))
                    wait(pe, gelu, b * UN + (u - 1))
                    product(u % 2, [w[:, e, :] for w in w1p], XFP[t]).then_inc(layer1, 1)
                there, b, u = behind(b, u, LAG_OUT)
                if not there:
                    return
                t, e = divmod(u, E)
                s = 2 + t % 2
                if e == 0:
                    wait(pe, fin, done(b, 0) if t == 2 else b * TH + (-1 if t and isinstance(b, int) and b == 0 else 0))
                    pe.wait_ge(loaded[t], (b + 1) * 64)
                    for a in range(2):
                        nc.tensor.matmul(psum[:, 2 * s + a, 0:CH], b2s[:], GR[t][:, a * CH:(a + 1) * CH],
                                         start=True, stop=False)
                pe.wait_ge(low, b * UN + (u + 1))
                product(s, [w[:, e, :] for w in w2p], HP[u % NH], before=True, close=(e == E - 1)).then_inc(layer2, 1)

            units(pe, step, LAG_OUT)

        @block.scalar
        def _(act):
            def step(b, u, late):
                if not late:
                    e = u % E
                    act.wait_ge(layer1, b * UN + (u + 1))
                    wait(act, low, b * UN + (u - NH + 1))
                    nc.scalar.activation(halves(Hd[u % NH][:]), slot(psum, u % 2), ACT.Gelu_apprx_tanh,
                                         bias=b1s[:, e:e + 1]).then_inc(gelu, 1)
                there, b, u = behind(b, u, LAG_PARTS)
                if not there:
                    return
                act.wait_ge(gated, b * UN + (u + 1))
                wait(act, layer2, b * UN + (u - NH + 1))
                nc.scalar.activation(HP[u % NH][0][:], Hd[u % NH][:], ACT.Copy).then_inc(high, 1)

            units(act, step, LAG_PARTS)

        @block.vector
        def _(dve):
            v = nc.vector

            def step(b0, u0, late):
                there, b, u = behind(b0, u0, LAG_FIN)
                if there and u % E == E - 1:
                    t = u // E
                    dve.wait_ge(layer2, b * UN + (u + 1))
                    dve.wait_ge(loaded[t], (b + 1) * 64)
                    wait(dve, stored[t], b * 16)
                    v.tensor_tensor(halves(OUT[t][:]), slot(psum, 2 + t % 2), halves(X2[t][:]), ALU.add).then_inc(fin, 1)
                if not late:
                    dve.wait_ge(gelu, b0 * UN + (u0 + 1))
                    dve.wait_ge(gates_spread, b0 * UN + (u0 + 1))
                    v.tensor_tensor(Hd[u0 % NH][:], Hd[u0 % NH][:], GB[u0 % NGB][:], ALU.mult).then_inc(gated, 1)
                there, b, u = behind(b0, u0, LAG_PARTS)
                if there:
                    dve.wait_ge(high, b * UN + (u + 1))
                    v.tensor_tensor(HP[u % NH][1][:], Hd[u % NH][:], HP[u % NH][0][:].bitcast(F32),
                                    ALU.subtract).then_inc(low, 1)

            units(dve, step, LAG_FIN)


def kernel(**inputs):
    import numpy as np
    import concourse.bacc as bacc
    from concourse.bass_utils import run_bass_kernel_spmd as run

    w = {n: np.asarray(a) for n, a in inputs.items()}
    p = {n.removeprefix("L0_conv_"): a for n, a in w.items() if n.startswith("L0_conv_")}
    f = {n.removeprefix("L0_ffn_"): a for n, a in w.items() if n.startswith("L0_ffn_")}
    f32 = np.float32

    def blocks(of, rows=DC, cols=DC):
        m = np.zeros((128, 128), f32)
        for k in range(KD):
            m[k * rows:(k + 1) * rows, k * cols:(k + 1) * cols] = of(k)
        return m

    m = {n: np.zeros((128, 128), f32) for n in MATS}
    m["IDENT"] = np.eye(128, dtype=f32)
    m["J128"] = np.full((128, 128), 1.0 / C, f32)
    m["J32"] = blocks(lambda k: f32(1.0 / DC))
    m["CEN128"] = m["IDENT"] - m["J128"]
    m["CEN32"] = m["IDENT"] - m["J32"]
    m["WZ"] = blocks(lambda k: p["Win"][k][:, DC:])
    m["WXT"] = blocks(lambda k: p["Wx"][k, :8], 8, DC)
    m["WDTT"] = blocks(lambda k: p["Wdt"][k].T, 8, DC)
    m["WB"] = blocks(lambda k: np.broadcast_to(p["Wx"][k, 8][:, None], (DC, DC)))
    m["WCC"] = blocks(lambda k: np.broadcast_to(p["Wx"][k, 9][:, None], (DC, DC)))
    m["WOUT"] = blocks(lambda k: p["Wout"][k])
    m["PROJ"] = p["proj_w"]
    m["FC2"][:R1] = p["fc2_w"]
    vecs = np.zeros((128, len(VECS)), f32)
    for i, n in enumerate(VECS):
        if n == "skip":
            vecs[:, i] = p["skip_scale"][0]
        elif n == "eps_in":
            vecs[:, i] = 1e-5 * 1e-6
        elif n == "eps_ln":
            vecs[:, i] = 1e-5
        else:
            flat = p[n].reshape(-1)
            vecs[:len(flat), i] = flat
    winx = np.tile(p["Win"][:, :, :DC].transpose(1, 0, 2), (3, 1, 1))
    taps = p["conv_w"][:, :, 0].transpose(2, 0, 3, 1)
    convw = np.repeat(taps, DC, axis=0)
    arrays = {
        "x": w["x"].reshape(B, C, L),
        "mats": np.stack([m[n] for n in MATS], axis=1),
        "vecs": vecs,
        "fc1": p["fc1_w"],
        "gate": f["gate_weight"],
        "winx": winx,
        "convw": convw,
        "w1": f["w1"].transpose(1, 0, 2),
        "b1": f["b1"].T,
        "w2": f["w2"].transpose(1, 0, 2),
        "b2": f["b2"],
    }
    arrays = {n: np.ascontiguousarray(a) for n, a in arrays.items()}
    nc = bacc.Bacc("TRN2", target_bir_lowering=False, num_devices=1)
    args = [nc.dram_tensor("in_" + n, a.shape, mybir.dt.from_np(a.dtype), kind="ExternalInput").ap()
            for n, a in arrays.items()]
    out = nc.dram_tensor("out", (B, C, L), F32, kind="ExternalOutput").ap()
    build_program(nc, *args, out)
    r = run(nc, [{"in_" + n: a for n, a in arrays.items()}], core_ids=[0])
    return r.results[0]["out"].reshape(B, C, HH, WW)
```

```python
from contextlib import ExitStack

import concourse.bass as bass
from concourse import mybir

ALU = mybir.AluOpType
ACT = mybir.ActivationFunctionType
AX_X = mybir.AxisListType.X
F32 = mybir.dt.float32
F32R = mybir.dt.float32r
U32 = mybir.dt.uint32

B, C, HH, WW = 16, 128, 48, 48
L = HH * WW
KD = 4
DC = C // KD
E, DFF = 16, 128
CAP = L // E * 2
R1 = C // 16
TH = 3
TL = L // TH
CH = TL // 2
CR = CH // WW
PW = WW + 2
PL = (HH + 2) * PW
SL = HH * PW
NT = L // 128
TT = TL // 128
BG = 128 // E
SOFTPLUS_MAX = 40.0

MATS = ["J128", "CEN128", "CEN32", "J32", "IDENT", "WZ", "WXT", "WDTT", "WB", "WCC", "WOUT", "PROJ", "FC2"]
VECS = ["norm_w", "norm_b", "conv_b", "dt_bias", "A_log", "Dp", "onorm_w", "onorm_b", "proj_b", "fc1_b", "fc2_b",
        "skip", "eps_in", "eps_ln"]


def build_program(nc, x, mats, vecs, fc1, gate, winx, convw, w1, b1, w2, b2, out):
    x2_dram = nc.dram_tensor("x2_dram", (B, C, L), F32).ap()
    xf_dram = nc.dram_tensor("xf_dram", (B, C, L), F32).ap()
    aff_dram = nc.dram_tensor("aff_dram", (B, E, L), F32).ap()
    gates_dram = nc.dram_tensor("gates_dram", (B, E, L), F32).ap()
    with ExitStack() as keep:
        def sb(name, shape, dt=F32):
            return keep.enter_context(nc.sbuf_tensor(name, shape, dt))

        psum = keep.enter_context(nc.psum_tensor("psum", [128, 8, 512], F32))
        route = Route(sb, keep.enter_context(nc.semaphore("search0")))
        mixer_phase(nc, psum, route, x, mats, vecs, fc1, gate, winx, convw, x2_dram, xf_dram, aff_dram)
        expert_phase(nc, psum, route, w1, w2, b1, b2, x2_dram, xf_dram, aff_dram, gates_dram, out)


def wait(eng, semaphore, value):
    if not isinstance(value, int) or value > 0:
        eng.wait_ge(semaphore, value)


def slot(psum, s):
    return psum[:, 2 * s:2 * s + 2, 0:CH]


def third(t):
    return slice(t * TL, (t + 1) * TL)


def halves(ap):
    return ap.rearrange("p (a n) -> p a n", a=2)


def done(b, t=TH - 1):
    return b * TH + (t + 1)


def in_order(k, image, c):
    if k % 2:
        image = image[:, ::-1, ::-1]
    if k >= 2:
        image = image.rearrange("p h w -> p w h")
    return image[:, c * CR:(c + 1) * CR, :]


class Route:

    BITS = 30
    STEP, INIT = 5, 2

    def __init__(self, sb, steps):
        self.steps = steps
        self.A = sb("affinities", [128, L])
        self.thr, self.cand, self.take, self.bit = (sb(n, [128, 1], U32) for n in ("thr", "cand", "take", "bit"))
        self.cnt = sb("cnt", [128, 1])

    def init(self, v, step):
        v.memset(self.thr[:], 0).then_inc(step, 1)
        v.memset(self.bit[:], 2 ** (self.BITS - 1)).then_inc(step, 1)

    def search(self, v, step, n, reached):
        base = n * self.STEP + self.INIT
        v.wait_ge(step, base)
        v.tensor_tensor(self.cand[:], self.thr[:], self.bit[:], ALU.bitwise_or).then_inc(step, 1)
        v.wait_ge(step, base + 1)
        v.tensor_scalar(reached, self.A[:], self.cand[:].bitcast(F32), 0.0, ALU.is_ge, ALU.add,
                        accum_out=self.cnt[:]).then_inc(step, 1)
        v.wait_ge(step, base + 2)
        v.tensor_scalar(self.take[:], self.cnt[:], float(CAP), self.bit[:], ALU.is_ge, ALU.mult).then_inc(step, 1)
        v.wait_ge(step, base + 3)
        v.tensor_tensor(self.thr[:], self.thr[:], self.take[:], ALU.bitwise_or).then_inc(step, 1)
        v.tensor_scalar(self.bit[:], self.bit[:], 1, None, ALU.logical_shift_right).then_inc(step, 1)

    def gates(self, v, step, n, W, Q, gated):
        A, cnt, t = self.A[:], self.cnt[:], self.thr[:].bitcast(F32)
        if n:
            v.wait_ge(step, n)
        v.tensor_scalar(W, A, t, 0.0, ALU.is_gt, ALU.add, accum_out=cnt).then_inc(step, 1)
        v.tensor_scalar(Q, A, t, None, ALU.is_equal).then_inc(step, 1)
        v.wait_ge(step, n + 2)
        v.tensor_scalar(cnt, cnt, -1.0, float(CAP), ALU.mult, ALU.add).then_inc(step, 1)
        v.tensor_tensor_scan(W, Q, Q, 0.0, ALU.add, ALU.max).then_inc(step, 1)
        v.wait_ge(step, n + 4)
        v.scalar_tensor_tensor(Q, W, cnt, Q, ALU.is_le, ALU.mult).then_inc(step, 1)
        v.wait_ge(step, n + 5)
        v.scalar_tensor_tensor(Q, A, t, Q, ALU.is_gt, ALU.add).then_inc(step, 1)
        v.wait_ge(step, n + 6)
        v.tensor_tensor(W, A, Q, ALU.mult).then_inc(gated, 1)


def mixer_phase(nc, psum, route, x, mats, vecs, fc1, gate, winx, convw, x2_dram, xf_dram, aff_dram):
    SEARCH_FROM = 10
    PER = route.BITS // (B - SEARCH_FROM)
    with ExitStack() as ctx:
        def sb(name, shape):
            return ctx.enter_context(nc.sbuf_tensor(name, shape, F32))

        def sem(name):
            return ctx.enter_context(nc.semaphore(name))

        m_all = sb("m_all", [128, len(MATS), 128])
        M = {n: m_all[:, i, :] for i, n in enumerate(MATS)}
        v_all = sb("v_all", [128, len(VECS)])
        V = {n: v_all[:, i:i + 1] for i, n in enumerate(VECS)}
        fc1s = sb("fc1s", [128, R1])
        gates = sb("gates", [128, E])
        winxs = sb("winxs", [96, KD, DC])
        convws = sb("convws", [96, KD, 3, DC])
        wconv = sb("wconv", [96, KD, 3, DC])
        wdelta = sb("wdelta", [128, 128])
        dpcen = sb("dpcen", [128, 128])
        projw = sb("projw", [128, 128])
        projc = sb("projc", [128, 128])
        vx = sb("vx", [128, 4])
        a_neg, fc2_neg, proj_c, a_exp = (vx[:, i:i + 1] for i in range(4))

        X = [sb(f"X{i}", [128, L]) for i in range(2)]
        XS = [sb(f"XS{i}", [128, PL]) for i in range(2)]
        zsum = [sb(f"zsum{i}", [128, TH]) for i in range(2)]
        stack = sb("stack", [96, KD, SL])
        SQ = sb("SQ", [128, L])
        RS = sb("RS", [128, L])
        U = sb("U", [128, L])
        ZS = sb("ZS", [128, L])
        CLXM = sb("CLXM", [128, L])
        DH = sb("DH", [128, L])
        DA = sb("DA", [128, L])
        DU = sb("DU", [128, L])
        G = sb("G", [128, L])
        XF = G
        X2 = sb("X2", [128, L])
        se1 = sb("se1", [R1, 1])
        sex = sb("sex", [128, 1])
        s1 = sb("s1", [128, 3])
        lg = sb("lg", [128, NT, E])
        aff = sb("aff", [128, NT, E])
        lgst = sb("lgst", [128, 3, NT])

        names = ("consts a_loaded border_zero prep_exp prep_vec prep_mm prep_done x_loaded stacked x2_stored xf_stored aff_stored "
                 "cen1_pe sq1 var1_pe ln1 rstd1 xn xs "
                 "conv_pe u z_pe zs fc1_pe relu1 fc2_pe sex_exp se_add se_done "
                 "pre_pe clamped sp_exp sp_ln delta du_pool decay bc_pe dbu cc_pe h hc "
                 "yc_pe sq2 var2_pe ln2 rstd2 yn g "
                 "out_pe xm cen3_pe sq3 var3_pe ln3 rstd3 proj_pe pr x2 "
                 "cen4_pe sq4 var4_pe ln4 rstd4 xf "
                 "lg_pe lg_max lg_sub lg_exp lg_sum lg_rec aff_ready afft_pe afft").split()
        S = {n: sem("m_" + n) for n in names}
        search = route.steps

        def run(eng, front, mid, tail, gate_of_last=None, begin_search=None):
            def pair(b0, searching, ends=False):
                for par in range(2):
                    b = b0 + par
                    last = ends and par == 1
                    mid(b, par, searching)
                    if not last:
                        front(b + 1, 1 - par)
                    tail(b, par, last, searching)

            front(0, 0)
            pair(0, False)
            if begin_search:
                with eng.Fori(1, SEARCH_FROM // 2) as i:
                    pair(i * 2, False)
                begin_search()
            with eng.Fori(SEARCH_FROM // 2 if begin_search else 1, B // 2 - 1) as i:
                pair(i * 2, True)
            pair(B - 2, True, ends=True)
            if gate_of_last:
                gate_of_last()

        def after_first(b):
            return not (isinstance(b, int) and b == 0)

        block = ctx.enter_context(nc.Block())

        @block.sync
        def _(sp):
            for dst, src in ((m_all[:], mats), (v_all[:], vecs), (fc1s[:], fc1), (gates[:], gate),
                             (winxs[:], winx), (convws[:], convw)):
                sp.dma_start(dst, src).then_inc(S["consts"], 16)

            def load(b, par):
                sp.dma_start(X[par][:], x[b]).then_inc(S["x_loaded"], 16)

            def front(b, par):
                wait(sp, S["xs"], done(b))
                wait(sp, S["conv_pe"], b * TH)
                for j in range(3):
                    for k in range(KD):
                        sp.dma_start(stack[DC * j:DC * j + DC, k, :],
                                     XS[par][DC * k:DC * k + DC, j * PW:j * PW + SL]).then_inc(S["stacked"], 16)

            def mid(b, par, searching):
                if not (isinstance(b, int) and b == B - 1):
                    wait(sp, S["x2"], b * TH)
                    load(b + 1, 1 - par)
                if after_first(b):
                    store_affinities(b)

            def tail(b, par, last, searching):
                wait(sp, S["x2"], done(b))
                sp.dma_start(x2_dram[b], X2[:]).then_inc(S["x2_stored"], 16)
                wait(sp, S["xf"], done(b))
                sp.dma_start(xf_dram[b], XF[:]).then_inc(S["xf_stored"], 16)

            def store_affinities(b):
                wait(sp, S["afft"], b * TH)
                sp.dma_start(aff_dram[b - 1], SQ[0:E, :]).then_inc(S["aff_stored"], 16)

            def begin_search():
                wait(sp, S["aff_stored"], 16 * (SEARCH_FROM - 1))
                sp.dma_start(route.A[:], aff_dram[0:BG].rearrange("b e n -> (b e) n")).then_inc(S["a_loaded"], 16)

            load(0, 0)
            run(sp, front, mid, tail, lambda: store_affinities(B), begin_search)
            for s in ("x2_stored", "xf_stored", "aff_stored"):
                wait(sp, S[s], 16 * B)

        @block.gpsimd
        def _(pool):
            for i in range(2):
                nc.gpsimd.memset(XS[i][:], 0.0).then_inc(S["border_zero"], 1)

            def front(b, par):
                pass

            def mid(b, par, searching):
                wait(pool, S["yc_pe"], b * TH)
                for t in range(TH):
                    wait(pool, S["delta"], done(b, t))
                    wait(pool, S["u"], done(b, t))
                    nc.gpsimd.tensor_tensor(DU[:, third(t)], DH[:, third(t)], U[:, third(t)],
                                            ALU.mult).then_inc(S["du_pool"], 1)

            def tail(b, par, last, searching):
                pass

            run(pool, front, mid, tail)

        @block.scalar
        def _(act):
            def rstd(ln, ps, b, t, out_sem, eps, scale=1.0):
                nc.scalar.activation(halves(RS[:, third(t)]), slot(psum, ps), ACT.Ln, bias=V[eps],
                                     scale=scale).then_inc(S[ln], 1)
                wait(act, S[ln], done(b, t))
                nc.scalar.activation(RS[:, third(t)], RS[:, third(t)], ACT.Exp, scale=-0.5).then_inc(S[out_sem], 1)

            act.preload_act_table_set("natural_log_exp_and_others")
            wait(act, S["consts"], 16 * 6)
            nc.scalar.activation(a_exp, V["A_log"], ACT.Exp).then_inc(S["prep_exp"], 1)
            wait(act, S["prep_done"], 3)
            wait(act, S["border_zero"], 2)

            def norm(squares, rstds):
                squares(0)
                squares(1)
                rstds(0)
                squares(2)
                rstds(1)
                rstds(2)

            def front(b, par):
                def squares(t):
                    wait(act, S["cen1_pe"], done(b, t))
                    if after_first(b):
                        wait(act, S["var2_pe"], done(b - 1, t))
                    nc.scalar.activation(halves(SQ[:, third(t)]), slot(psum, 1 + t), ACT.Square).then_inc(S["sq1"], 1)

                def rstds(t):
                    wait(act, S["var1_pe"], done(b, t))
                    if after_first(b):
                        wait(act, S["yn"], done(b - 1, t))
                    rstd("ln1", 0, b, t, "rstd1", "eps_in", 1.0 + 1e-5)

                norm(squares, rstds)
                for t in range(TH):
                    wait(act, S["xn"], done(b, t))
                    view = XS[par][:].rearrange("p (h w) -> p h w", w=PW)[:, 1 + 16 * t:17 + 16 * t, 1:1 + WW]
                    nc.scalar.activation(view, view, ACT.Identity, bias=V["norm_b"],
                                         accum_out=zsum[par][:, t:t + 1]).then_inc(S["xs"], 1)

            def exp_logits(b):
                wait(act, S["lg_sub"], b)
                nc.scalar.activation(lg[:], lg[:], ACT.Exp).then_inc(S["lg_exp"], 1)

            def copy_affinities(b, t):
                wait(act, S["afft_pe"], done(b - 1, t))
                wait(act, S["var4_pe"], b * TH)
                nc.scalar.activation(halves(SQ[0:E, third(t)]), slot(psum, 2)[0:E], ACT.Copy).then_inc(S["afft"], 1)

            def mid(b, par, searching):
                wait(act, S["yc_pe"], b * TH)
                for t in range(TH):
                    wait(act, S["conv_pe"], done(b, t))
                    nc.scalar.activation(halves(U[:, third(t)]), slot(psum, t), ACT.Silu,
                                         bias=V["conv_b"]).then_inc(S["u"], 1)
                wait(act, S["g"], b * TH)
                for t in range(TH):
                    wait(act, S["z_pe"], done(b, t))
                    nc.scalar.activation(halves(ZS[:, third(t)]), slot(psum, (3, 0, 1)[t]),
                                         ACT.Silu).then_inc(S["zs"], 1)
                act.preload_act_table_set("natural_log_exp_and_others")
                wait(act, S["fc1_pe"], b + 1)
                nc.scalar.activation(se1[:], psum[0:R1, 4, 0:1], ACT.Relu, bias=V["fc1_b"][0:R1],
                                     scale=1.0 / L).then_inc(S["relu1"], 1)
                for t in range(TH):
                    wait(act, S["clamped"], done(b, t))
                    nc.scalar.activation(CLXM[:, third(t)], CLXM[:, third(t)], ACT.Exp).then_inc(S["sp_exp"], 1)
                    wait(act, S["sp_exp"], done(b, t))
                    nc.scalar.activation(CLXM[:, third(t)], CLXM[:, third(t)], ACT.Ln, bias=1.0).then_inc(S["sp_ln"], 1)
                if after_first(b):
                    exp_logits(b)
                wait(act, S["fc2_pe"], b + 1)
                nc.scalar.activation(sex[:], psum[:, 4, 0:1], ACT.Exp, bias=fc2_neg, scale=-1.0).then_inc(S["sex_exp"], 1)
                wait(act, S["h"], b * TH)
                for t in range(TH):
                    wait(act, S["delta"], done(b, t))
                    nc.scalar.activation(DA[:, third(t)], DH[:, third(t)], ACT.Exp, scale=a_neg).then_inc(S["decay"], 1)
                    if after_first(b):
                        copy_affinities(b, t)
                wait(act, S["var4_pe"], b * TH)
                wait(act, S["aff_stored"], b * 16)
                wait(act, S["xf"], b * TH)

                def squares(t):
                    wait(act, S["yc_pe"], done(b, t))
                    nc.scalar.activation(halves(SQ[:, third(t)]), slot(psum, 1 + t), ACT.Square).then_inc(S["sq2"], 1)

                def rstds(t):
                    wait(act, S["var2_pe"], done(b, t))
                    rstd("ln2", 0, b, t, "rstd2", "eps_ln")

                norm(squares, rstds)

            def tail(b, par, last, searching):
                for t in range(TH):
                    wait(act, S["cen3_pe"], done(b, t))
                    wait(act, *((S["var2_pe"], done(b, t)) if last else (S["var1_pe"], done(b + 1, t))))
                    nc.scalar.activation(halves(SQ[:, third(t)]), slot(psum, t), ACT.Square).then_inc(S["sq3"], 1)
                for t in range(TH):
                    wait(act, S["var3_pe"], done(b, t))
                    wait(act, *((S["yn"], done(b, t)) if last else (S["xn"], done(b + 1, t))))
                    rstd("ln3", (3, 0, 1)[t], b, t, "rstd3", "eps_ln")

                def squares(t):
                    wait(act, S["cen4_pe"], done(b, t))
                    wait(act, S["var3_pe"], done(b, t))
                    nc.scalar.activation(halves(SQ[:, third(t)]), slot(psum, 1 + t), ACT.Square).then_inc(S["sq4"], 1)

                def rstds(t):
                    wait(act, S["var4_pe"], done(b, t))
                    wait(act, S["pr"], done(b, t))
                    rstd("ln4", 0, b, t, "rstd4", "eps_ln")

                norm(squares, rstds)

            def gate_of_last():
                exp_logits(B)
                for t in range(TH):
                    copy_affinities(B, t)

            run(act, front, mid, tail, gate_of_last)

        @block.vector
        def _(dve):
            v = nc.vector
            wait(dve, S["consts"], 16 * 6)
            for dx in range(3):
                v.tensor_tensor(wconv[:, :, dx, :], winxs[:], convws[:, :, dx, :], ALU.mult).then_inc(S["prep_vec"], 1)
            v.tensor_scalar(dpcen[:], M["CEN32"], V["Dp"], None, ALU.mult).then_inc(S["prep_vec"], 1)
            v.tensor_scalar(projw[:], M["PROJ"], V["norm_w"], None, ALU.mult).then_inc(S["prep_vec"], 1)
            v.tensor_scalar(fc2_neg, V["fc2_b"], -1.0, None, ALU.mult).then_inc(S["prep_vec"], 1)
            wait(dve, S["prep_exp"], 1)
            v.tensor_scalar(a_neg, a_exp, -1.0, None, ALU.mult).then_inc(S["prep_vec"], 1)
            wait(dve, S["prep_mm"], 3)
            v.tensor_copy(wdelta[:], psum[:, 0, 0:128]).then_inc(S["prep_done"], 1)
            v.tensor_copy(projc[:], psum[:, 2, 0:128]).then_inc(S["prep_done"], 1)
            v.tensor_tensor(proj_c, psum[:, 4, 0:1], V["proj_b"], ALU.add).then_inc(S["prep_done"], 1)
            wait(dve, S["prep_vec"], 7)
            wait(dve, S["prep_done"], 3)
            wait(dve, S["border_zero"], 2)

            def interior(par, t):
                return XS[par][:].rearrange("p (h w) -> p h w", w=PW)[:, 1 + 16 * t:17 + 16 * t, 1:1 + WW]

            def rows(ap):
                return ap.rearrange("p (a h w) -> p a h w", a=2, w=WW)

            def ps_rows(s):
                return slot(psum, s).rearrange("p a (h w) -> p a h w", w=WW)

            def front(b, par):
                for t in range(TH):
                    wait(dve, S["rstd1"], done(b, t))
                    v.scalar_tensor_tensor(interior(par, t).rearrange("p (a h) w -> p a h w", a=2), ps_rows(1 + t),
                                           V["norm_w"], rows(RS[:, third(t)]), ALU.mult, ALU.mult).then_inc(S["xn"], 1)

            def mid(b, par, searching):
                if searching:
                    for n in range(PER - 2):
                        search_step(b, n)
                wait(dve, S["proj_pe"], b * TH)
                for t in range(TH):
                    wait(dve, S["pre_pe"], done(b, t))
                    v.tensor_scalar(halves(CLXM[:, third(t)]), slot(psum, (3, 0, 1)[t]), V["dt_bias"], SOFTPLUS_MAX,
                                    ALU.add, ALU.min).then_inc(S["clamped"], 1)
                if after_first(b):
                    shift_logits(b)
                wait(dve, S["yc_pe"], b * TH)
                for t in range(TH):
                    wait(dve, S["sp_ln"], done(b, t))
                    v.scalar_tensor_tensor(halves(DH[:, third(t)]), slot(psum, (3, 0, 1)[t]), V["dt_bias"],
                                           halves(CLXM[:, third(t)]), ALU.add, ALU.max).then_inc(S["delta"], 1)
                if after_first(b):
                    affinities(b)

                def dbu(t):
                    wait(dve, S["bc_pe"], done(b, t))
                    wait(dve, S["du_pool"], done(b, t))
                    v.tensor_tensor(halves(DU[:, third(t)]), halves(DU[:, third(t)]), slot(psum, (3, 0, 1)[t]),
                                    ALU.mult).then_inc(S["dbu"], 1)

                def scan(t):
                    wait(dve, S["decay"], done(b, t))
                    wait(dve, S["dbu"], done(b, t))
                    if t:
                        wait(dve, S["h"], done(b, t - 1))
                    v.tensor_tensor_scan(DH[:, third(t)], DA[:, third(t)], DU[:, third(t)],
                                         DH[:, t * TL - 1:t * TL] if t else 0.0, ALU.mult, ALU.add).then_inc(S["h"], 1)

                def hc(t):
                    wait(dve, S["cc_pe"], done(b, t))
                    wait(dve, S["h"], done(b, t))
                    v.tensor_tensor(halves(DU[:, third(t)]), halves(DH[:, third(t)]), slot(psum, (2, 3, 0)[t]),
                                    ALU.mult).then_inc(S["hc"], 1)

                dbu(0)
                scan(0)
                dbu(1)
                hc(0)
                scan(1)
                dbu(2)
                hc(1)
                scan(2)
                hc(2)
                wait(dve, S["sex_exp"], b + 1)
                wait(dve, S["xm"], b * TH)
                v.tensor_scalar(s1[:, 0:1], sex[:], 1.0, None, ALU.add).then_inc(S["se_add"], 1)
                wait(dve, S["se_add"], b * 2 + 1)
                v.reciprocal(s1[:, 1:2], s1[:, 0:1]).then_inc(S["se_add"], 1)
                wait(dve, S["se_add"], b * 2 + 2)
                v.tensor_tensor(s1[:, 2:3], s1[:, 1:2], V["skip"], ALU.mult).then_inc(S["se_done"], 1)
                wait(dve, S["xf_stored"], b * 16)
                wait(dve, S["lg_pe"], b)
                for t in range(TH):
                    wait(dve, S["rstd2"], done(b, t))
                    v.scalar_tensor_tensor(halves(G[:, third(t)]), slot(psum, 1 + t), V["onorm_w"], halves(RS[:, third(t)]),
                                           ALU.mult, ALU.mult).then_inc(S["yn"], 1)
                    wait(dve, S["yn"], done(b, t))
                    wait(dve, S["zs"], done(b, t))
                    v.scalar_tensor_tensor(G[:, third(t)], G[:, third(t)], V["onorm_b"], ZS[:, third(t)],
                                           ALU.add, ALU.mult).then_inc(S["g"], 1)

            def tail(b, par, last, searching):
                wait(dve, S["se_done"], b + 1)
                for t in range(TH):
                    wait(dve, S["out_pe"], done(b, t))
                    v.scalar_tensor_tensor(rows(CLXM[:, third(t)]), interior(par, t).rearrange("p (a h) w -> p a h w", a=2),
                                           s1[:, 2:3], ps_rows(1 + t), ALU.mult, ALU.mult).then_inc(S["xm"], 1)
                if searching:
                    search_step(b, PER - 2)
                wait(dve, S["x2_stored"], b * 16)
                wait(dve, S["cen4_pe"], b * TH)
                for t in range(TH):
                    wait(dve, S["proj_pe"], done(b, t))
                    wait(dve, S["rstd3"], done(b, t))
                    v.tensor_tensor(halves(X2[:, third(t)]), slot(psum, (2, 3, 0)[t]), halves(RS[:, third(t)]),
                                    ALU.mult).then_inc(S["pr"], 1)
                    wait(dve, S["pr"], done(b, t))
                    v.scalar_tensor_tensor(X2[:, third(t)], X2[:, third(t)], proj_c, X[par][:, third(t)],
                                           ALU.add, ALU.add).then_inc(S["x2"], 1)
                if searching:
                    search_step(b, PER - 1)
                wait(dve, S["out_pe"], done(b))
                for t in range(TH):
                    wait(dve, S["rstd4"], done(b, t))
                    v.tensor_tensor(halves(XF[:, third(t)]), slot(psum, 1 + t), halves(RS[:, third(t)]),
                                    ALU.mult).then_inc(S["xf"], 1)

            def shift_logits(b):
                wait(dve, S["lg_pe"], b)
                lp = psum[:, 4, 0:NT * E].rearrange("p (t e) -> p t e", e=E)
                v.tensor_reduce(lgst[:, 0, :], lp, AX_X, ALU.max).then_inc(S["lg_max"], 1)
                wait(dve, S["lg_max"], b)
                v.tensor_tensor(lg[:], lp, lgst[:, 0, :].unsqueeze(2).to_broadcast([128, NT, E]),
                                ALU.subtract).then_inc(S["lg_sub"], 1)

            def affinities(b):
                wait(dve, S["lg_exp"], b)
                v.tensor_reduce(lgst[:, 1, :], lg[:], AX_X, ALU.add).then_inc(S["lg_sum"], 1)
                wait(dve, S["lg_sum"], b)
                v.reciprocal(lgst[:, 2, :], lgst[:, 1, :]).then_inc(S["lg_rec"], 1)
                wait(dve, S["lg_rec"], b)
                wait(dve, S["afft_pe"], (b - 1) * TH)
                v.tensor_tensor(aff[:], lg[:], lgst[:, 2, :].unsqueeze(2).to_broadcast([128, NT, E]),
                                ALU.mult).then_inc(S["aff_ready"], 1)

            def begin_search():
                route.init(v, search)
                wait(dve, S["a_loaded"], 16)

            def search_step(b, n):
                route.search(v, search, (b - SEARCH_FROM) * PER + n, DA[:])

            def gate_of_last():
                shift_logits(B)
                affinities(B)

            run(dve, front, mid, tail, gate_of_last, begin_search)

        @block.tensor
        def _(pe):
            mm = nc.tensor.matmul

            def full(s, w, src, t):
                for a in range(2):
                    last = mm(psum[:, 2 * s + a, 0:CH], w, src[:, t * TL + a * CH:t * TL + (a + 1) * CH],
                              start=True, stop=True)
                return last

            wait(pe, S["consts"], 16 * 6)
            wait(pe, S["prep_vec"], 7)
            mm(psum[:, 0, 0:128], M["WXT"][0:32], M["WDTT"][0:32], start=True, stop=True).then_inc(S["prep_mm"], 1)
            mm(psum[:, 2, 0:128], M["CEN128"], projw[:], start=True, stop=True).then_inc(S["prep_mm"], 1)
            mm(psum[:, 4, 0:1], M["PROJ"], V["norm_b"], start=True, stop=True).then_inc(S["prep_mm"], 1)
            wait(pe, S["prep_done"], 3)

            def norm(centre, variance):
                centre(0)
                centre(1)
                variance(0)
                centre(2)
                variance(1)
                variance(2)

            def front(b, par):
                wait(pe, S["x_loaded"], b * 16 + 16)

                def centre(t):
                    if after_first(b):
                        wait(pe, S["yn"], done(b - 1, t))
                    full(1 + t, M["CEN128"], X[par], t).then_inc(S["cen1_pe"], 1)

                def variance(t):
                    wait(pe, S["sq1"], done(b, t))
                    if t:
                        wait(pe, S["ln1"], done(b, t - 1))
                    elif after_first(b):
                        wait(pe, S["ln2"], done(b - 1))
                    full(0, M["J128"], SQ, t).then_inc(S["var1_pe"], 1)

                norm(centre, variance)

            def logits(b):
                wait(pe, S["xf"], b * TH)
                for n in range(NT):
                    last = mm(psum[:, 4, n * E:(n + 1) * E], XF[:, n * 128:(n + 1) * 128], gates[:], start=True, stop=True)
                last.then_inc(S["lg_pe"], 1)

            def transpose_affinities(b, t):
                wait(pe, S["aff_ready"], b)
                if t:
                    wait(pe, S["afft"], done(b - 1, t - 1))
                for n in range(TT):
                    bank, col = 4 + n // 3, n % 3 * 128
                    last = nc.tensor.transpose(psum[0:E, bank, col:col + 128], aff[:, t * TT + n, :], M["IDENT"])
                last.then_inc(S["afft_pe"], 1)

            def mid(b, par, searching):
                wait(pe, S["stacked"], (b + 1) * (3 * KD * 16))
                for t in range(TH):
                    if t == 0:
                        wait(pe, S["ln4"], b * TH)
                    elif after_first(b):
                        wait(pe, S["xf"], done(b - 1, t - 1))
                    for a in range(2):
                        for dx in range(3):
                            for k in range(KD):
                                img = stack[:, k, :].rearrange("p (h w) -> p h w", w=PW)[:, :, dx:dx + WW]
                                last = mm(psum[32 * k:32 * k + 32, 2 * t + a, 0:CH], wconv[:, k, dx, :],
                                          in_order(k, img, 2 * t + a), start=(dx == 0), stop=(dx == 2))
                    last.then_inc(S["conv_pe"], 1)
                for t in range(TH):
                    s = (3, 0, 1)[t]
                    if t == 0:
                        wait(pe, S["xf"], b * TH)
                    else:
                        wait(pe, S["u"], done(b, t - 1))
                    for a in range(2):
                        for k in range(KD):
                            img = XS[par][:].rearrange("p (h w) -> p h w", w=PW)[:, 1:1 + HH, 1:1 + WW]
                            last = mm(psum[32 * k:32 * k + 32, 2 * s + a, 0:CH], M["WZ"][:, 32 * k:32 * k + 32],
                                      in_order(k, img, 2 * t + a), start=True, stop=True)
                    last.then_inc(S["z_pe"], 1)
                wait(pe, S["u"], done(b))
                for t in range(TH):
                    last = mm(psum[0:R1, 4, 0:1], fc1s[:], zsum[par][:, t:t + 1], start=(t == 0), stop=(t == TH - 1))
                last.then_inc(S["fc1_pe"], 1)
                for t in range(TH):
                    wait(pe, S["zs"], done(b, t))
                    full((3, 0, 1)[t], wdelta[:], U, t).then_inc(S["pre_pe"], 1)
                    if t == 0:
                        wait(pe, S["relu1"], b + 1)
                        if after_first(b):
                            logits(b)
                wait(pe, S["lg_sub"], b)
                mm(psum[:, 4, 0:1], M["FC2"][0:R1], se1[:], start=True, stop=True).then_inc(S["fc2_pe"], 1)
                for t in range(TH):
                    wait(pe, S["delta"], done(b, t))
                    full((3, 0, 1)[t], M["WB"], U, t).then_inc(S["bc_pe"], 1)
                    if t == 0:
                        wait(pe, S["sex_exp"], b + 1)
                    if after_first(b):
                        transpose_affinities(b, t)
                for t in range(TH):
                    if t == 0:
                        wait(pe, S["afft"], b * TH)
                    else:
                        wait(pe, S["dbu"], done(b, t - 1))
                    full((2, 3, 0)[t], M["WCC"], U, t).then_inc(S["cc_pe"], 1)

                def centre(t):
                    if t == 0:
                        wait(pe, S["dbu"], done(b))
                    wait(pe, S["hc"], done(b, t))
                    for a in range(2):
                        cols = slice(t * TL + a * CH, t * TL + (a + 1) * CH)
                        mm(psum[:, 2 * (1 + t) + a, 0:CH], M["CEN32"], DU[:, cols], start=True, stop=False)
                        last = mm(psum[:, 2 * (1 + t) + a, 0:CH], dpcen[:], U[:, cols], start=False, stop=True)
                    last.then_inc(S["yc_pe"], 1)

                def variance(t):
                    wait(pe, S["sq2"], done(b, t))
                    if t == 0:
                        wait(pe, S["hc"], done(b))
                    else:
                        wait(pe, S["ln2"], done(b, t - 1))
                    full(0, M["J32"], SQ, t).then_inc(S["var2_pe"], 1)

                norm(centre, variance)

            def tail(b, par, last_image, searching):
                wait(pe, S["g"], done(b))
                for t in range(TH):
                    wait(pe, *((S["yn"], done(b, t)) if last_image else (S["xn"], done(b + 1, t))))
                    for a in range(2):
                        for k in range(KD):
                            seq = G[:].rearrange("p (h w) -> p h w", w=WW)
                            last = mm(psum[32 * k:32 * k + 32, 2 * (1 + t) + a, 0:CH], M["WOUT"][:, 32 * k:32 * k + 32],
                                      in_order(k, seq, 2 * t + a), start=True, stop=True)
                    last.then_inc(S["out_pe"], 1)
                wait(pe, *((S["ln2"], done(b)) if last_image else (S["ln1"], done(b + 1))))
                for t in range(TH):
                    wait(pe, S["xm"], done(b, t))
                    full(t, M["CEN128"], CLXM, t).then_inc(S["cen3_pe"], 1)
                for t in range(TH):
                    wait(pe, S["sq3"], done(b, t))
                    full((3, 0, 1)[t], M["J128"], SQ, t).then_inc(S["var3_pe"], 1)
                for t in range(TH):
                    if t:
                        wait(pe, S["ln3"], done(b, t - 1))
                    full((2, 3, 0)[t], projc[:], CLXM, t).then_inc(S["proj_pe"], 1)

                def centre(t):
                    if t == 0:
                        wait(pe, S["ln3"], done(b))
                    wait(pe, S["x2"], done(b, t))
                    full(1 + t, M["CEN128"], X2, t).then_inc(S["cen4_pe"], 1)

                def variance(t):
                    wait(pe, S["sq4"], done(b, t))
                    if t == 0:
                        wait(pe, S["pr"], done(b))
                    else:
                        wait(pe, S["ln4"], done(b, t - 1))
                    full(0, M["J128"], SQ, t).then_inc(S["var4_pe"], 1)

                norm(centre, variance)

            def gate_of_last():
                logits(B)
                for t in range(TH):
                    if t == 0:
                        wait(pe, S["lg_sub"], B)
                    transpose_affinities(B, t)

            run(pe, front, mid, tail, gate_of_last)


def expert_phase(nc, psum, route, w1, w2, b1, b2, x2_dram, xf_dram, aff_dram, gates_dram, out):
    UN = TH * E
    SEARCHED = 6
    PER = Route.BITS // SEARCHED
    LAG_PARTS = 1
    LAG_OUT = 3
    LAG_FIN = 4
    NH, NGB = 4, 3
    with ExitStack() as ctx:
        def sb(name, shape, dt=F32):
            return ctx.enter_context(nc.sbuf_tensor(name, shape, dt))

        def sem(name):
            return ctx.enter_context(nc.semaphore(name))

        w1p = [sb(f"w1p{i}", [128, E, DFF], F32R) for i in range(2)]
        w2p = [sb(f"w2p{i}", [128, E, C], F32R) for i in range(2)]
        b1s = sb("b1s", [128, E])
        b2s = sb("b2s", [E, C])
        W, Q = sb("W", [128, L]), sb("Q", [128, L])
        XF = [sb(f"xf{t}", [128, TL]) for t in range(TH)]
        XFP = [[sb(f"xfp{t}_{i}", [128, TL], F32R) for i in range(2)] for t in range(TH)]
        X2 = [sb(f"x2{t}", [128, TL]) for t in range(TH)]
        GR = [sb(f"gr{t}", [E, TL]) for t in range(TH)]
        GQ = [sb(f"gq{t}", [128, E // 4, TL]) for t in range(TH)]
        Hd_all = sb("hd_all", [128, NH, TL])
        Hd = [Hd_all[:, i, :] for i in range(NH)]
        HP = [[sb(f"hp{i}_{j}", [128, TL], F32R) for j in range(2)] for i in range(NH)]
        whole = Hd_all[:].rearrange("p a n -> p (a n)")[:, 0:E * 128].rearrange("p (e n) -> p e n", e=E)
        GB = [sb(f"gb{i}", [128, TL]) for i in range(NGB)]
        loaded, stored = [sem(f"e_loaded{t}") for t in range(TH)], [sem(f"e_stored{t}") for t in range(TH)]
        pool_turn = sem("e_pool_turn")
        w_loaded, b_loaded, w_high, w_low = (sem("e_" + n) for n in ("w_loaded", "b_loaded", "w_high", "w_low"))
        a_loaded, gates_ready, gates_stored = sem("e_a_loaded"), sem("e_gates_ready"), sem("e_gates_stored")
        search1 = sem("e_search1")
        xf_high, xf_split, layer1, gelu, gates_spread, gated, high, low, layer2, fin = (
            sem("e_" + n) for n in ("xf_high", "xf_split", "layer1", "gelu", "gates_spread", "gated", "high", "low", "layer2", "fin"))
        block = ctx.enter_context(nc.Block())

        def units(eng, step, lag):
            for u in range(UN):
                step(0, u, False)
            with eng.Fori(1, B) as b:
                for u in range(UN):
                    step(b, u, False)
            for u in range(lag):
                step(B, u, True)

        def behind(b, u, lag):
            if u >= lag:
                return not (isinstance(b, int) and b == B), b, u - lag
            return not (isinstance(b, int) and b == 0), b - 1, u - lag + UN

        @block.sync
        def _(sp):
            def load(b, t):
                sp.dma_start(XF[t][:], xf_dram[b, :, third(t)]).then_inc(loaded[t], 16)
                sp.dma_start(GQ[t][0:97:32, :, :],
                             gates_dram[b, :, third(t)].rearrange("(q j) n -> q j n", q=4)).then_inc(loaded[t], 16)
                sp.dma_start(GR[t][:], gates_dram[b, :, third(t)]).then_inc(loaded[t], 16)
                sp.dma_start(X2[t][:], x2_dram[b, :, third(t)]).then_inc(loaded[t], 16)

            def store(b, t):
                sp.wait_ge(fin, done(b, t))
                sp.dma_start(out[b, :, third(t)], X2[t][:]).then_inc(stored[t], 16)

            def images(first, end):
                with sp.Fori(first, end) as b:
                    for t in range(TH):
                        store(b - 1, t)
                        sp.wait_ge(stored[t], b * 16)
                        load(b, t)

            def gates(g):
                sp.wait_ge(gates_ready, g + 1)
                sp.dma_start(gates_dram[g * BG:(g + 1) * BG].rearrange("b e n -> (b e) n"), W[:]).then_inc(gates_stored, 16)

            for n, w in enumerate((w1, w2)):
                if n:
                    sp.wait_ge(w_low, n)
                sp.dma_start(whole, w).then_inc(w_loaded, 16)
            sp.dma_start(b1s[:], b1).then_inc(b_loaded, 16)
            sp.dma_start(b2s[:], b2).then_inc(b_loaded, 16)
            gates(0)
            sp.dma_start(route.A[:], aff_dram[BG:B].rearrange("b e n -> (b e) n")).then_inc(a_loaded, 16)
            sp.wait_ge(gates_stored, 16)
            for t in range(TH):
                load(0, t)
            images(1, BG - 1)
            gates(1)
            sp.wait_ge(gates_stored, 32)
            images(BG - 1, B)
            for t in range(TH):
                store(B - 1, t)
            for t in range(TH):
                sp.wait_ge(stored[t], 16 * B)

        @block.gpsimd
        def _(pool):
            def step(b, u, late):
                t, e = divmod(u, E)
                if e == 0:
                    pool.wait_ge(loaded[t], (b + 1) * 64)
                    wait(pool, gates_spread, b * UN + u)
                    pool.sem_inc(pool_turn, 1)
                    nc.gpsimd.tensor_copy(XFP[t][0][:], XF[t][:]).then_inc(xf_high, 1)
                    pool.wait_ge(xf_high, done(b, t))
                    nc.gpsimd.tensor_tensor(XFP[t][1][:], XF[t][:], XFP[t][0][:].bitcast(F32),
                                            ALU.subtract).then_inc(xf_split, 1)
                    pool.wait_ge(xf_split, done(b, t))
                wait(pool, gated, b * UN + (u - NGB + 1))
                pool.sem_inc(pool_turn, 1)
                q, j = divmod(e, 4)
                nc.gpsimd.partition_broadcast(GB[u % NGB][:], GQ[t][32 * q:32 * q + 1, j, :]).then_inc(gates_spread, 1)

            for n, parts in enumerate((w1p, w2p)):
                pool.wait_ge(w_high, n + 1)
                nc.gpsimd.tensor_tensor(parts[1][:], whole, parts[0][:].bitcast(F32), ALU.subtract).then_inc(w_low, 1)
            units(pool, step, 0)

        @block.tensor
        def _(pe):
            def product(s, weights, parts, before=False, **flags):
                passes = [(0, 0), (0, 1), (1, 0)]
                for n, (i, j) in enumerate(passes):
                    for a in range(2):
                        last = nc.tensor.matmul(psum[:, 2 * s + a, 0:CH], weights[i], parts[j][:, a * CH:(a + 1) * CH],
                                                start=(n == 0 and not before), stop=(n == 2 and flags.get("close", True)))
                return last

            def step(b, u, late):
                if not late:
                    t, e = divmod(u, E)
                    if e == 0:
                        pe.wait_ge(xf_split, done(b, t))
                    wait(pe, gelu, b * UN + (u - 1))
                    product(u % 2, [w[:, e, :] for w in w1p], XFP[t]).then_inc(layer1, 1)
                there, b, u = behind(b, u, LAG_OUT)
                if not there:
                    return
                t, e = divmod(u, E)
                s = 2 + t % 2
                if e == 0:
                    wait(pe, fin, done(b, 0) if t == 2 else b * TH + (-1 if t and isinstance(b, int) and b == 0 else 0))
                    pe.wait_ge(loaded[t], (b + 1) * 64)
                    for a in range(2):
                        nc.tensor.matmul(psum[:, 2 * s + a, 0:CH], b2s[:], GR[t][:, a * CH:(a + 1) * CH],
                                         start=True, stop=False)
                pe.wait_ge(low, b * UN + (u + 1))
                product(s, [w[:, e, :] for w in w2p], HP[u % NH], before=True, close=(e == E - 1)).then_inc(layer2, 1)

            pe.wait_ge(b_loaded, 32)
            pe.wait_ge(w_low, 2)
            units(pe, step, LAG_OUT)

        @block.scalar
        def _(act):
            def step(b, u, late):
                if not late:
                    e = u % E
                    act.wait_ge(layer1, b * UN + (u + 1))
                    wait(act, low, b * UN + (u - NH + 1))
                    nc.scalar.activation(halves(Hd[u % NH]), slot(psum, u % 2), ACT.Gelu_apprx_tanh,
                                         bias=b1s[:, e:e + 1]).then_inc(gelu, 1)
                there, b, u = behind(b, u, LAG_PARTS)
                if not there:
                    return
                act.wait_ge(gated, b * UN + (u + 1))
                wait(act, layer2, b * UN + (u - NH + 1))
                nc.scalar.activation(HP[u % NH][0][:], Hd[u % NH], ACT.Copy).then_inc(high, 1)

            for n, parts in enumerate((w1p, w2p)):
                act.wait_ge(w_loaded, 16 * (n + 1))
                nc.scalar.activation(parts[0][:], whole, ACT.Copy).then_inc(w_high, 1)
            act.wait_ge(b_loaded, 32)
            act.wait_ge(w_low, 2)
            units(act, step, LAG_PARTS)

        @block.vector
        def _(dve):
            v = nc.vector

            def step(b0, u0, late):
                there, b, u = behind(b0, u0, LAG_FIN)
                if there and u % E == E - 1:
                    t = u // E
                    dve.wait_ge(layer2, b * UN + (u + 1))
                    dve.wait_ge(loaded[t], (b + 1) * 64)
                    v.tensor_tensor(halves(X2[t][:]), slot(psum, 2 + t % 2), halves(X2[t][:]), ALU.add).then_inc(fin, 1)
                if not late:
                    dve.wait_ge(gelu, b0 * UN + (u0 + 1))
                    dve.wait_ge(gates_spread, b0 * UN + (u0 + 1))
                    v.tensor_tensor(Hd[u0 % NH], Hd[u0 % NH], GB[u0 % NGB][:], ALU.mult).then_inc(gated, 1)
                there, b, u = behind(b0, u0, LAG_PARTS)
                if there:
                    dve.wait_ge(high, b * UN + (u + 1))
                    v.tensor_tensor(HP[u % NH][1][:], Hd[u % NH], HP[u % NH][0][:].bitcast(F32),
                                    ALU.subtract).then_inc(low, 1)

            def image(b, searching=False):
                for u in range(UN):
                    step(b, u, False)
                    n, at = divmod(u, UN // PER)
                    if searching and at == 4 and n < PER:
                        route.search(v, search1, b * PER + n, Q[:])

            route.gates(v, route.steps, Route.INIT + Route.BITS * Route.STEP, W[:], Q[:], gates_ready)
            route.init(v, search1)
            dve.wait_ge(gates_ready, 1)
            dve.wait_ge(a_loaded, 16)
            image(0, searching=True)
            with dve.Fori(1, SEARCHED) as b:
                image(b, searching=True)
            dve.wait_ge(gates_stored, 16)
            route.gates(v, search1, Route.INIT + Route.BITS * Route.STEP, W[:], Q[:], gates_ready)
            with dve.Fori(SEARCHED, B) as b:
                image(b)
            for u in range(LAG_FIN):
                step(B, u, True)


def kernel(**inputs):
    import numpy as np
    import concourse.bacc as bacc
    from concourse.bass_utils import run_bass_kernel_spmd as run

    w = {n: np.asarray(a) for n, a in inputs.items()}
    p = {n.removeprefix("L0_conv_"): a for n, a in w.items() if n.startswith("L0_conv_")}
    f = {n.removeprefix("L0_ffn_"): a for n, a in w.items() if n.startswith("L0_ffn_")}
    f32 = np.float32

    def blocks(of, rows=DC, cols=DC):
        m = np.zeros((128, 128), f32)
        for k in range(KD):
            m[k * rows:(k + 1) * rows, k * cols:(k + 1) * cols] = of(k)
        return m

    m = {n: np.zeros((128, 128), f32) for n in MATS}
    m["IDENT"] = np.eye(128, dtype=f32)
    m["J128"] = np.full((128, 128), 1.0 / C, f32)
    m["J32"] = blocks(lambda k: f32(1.0 / DC))
    m["CEN128"] = m["IDENT"] - m["J128"]
    m["CEN32"] = m["IDENT"] - m["J32"]
    m["WZ"] = blocks(lambda k: p["Win"][k][:, DC:])
    m["WXT"] = blocks(lambda k: p["Wx"][k, :8], 8, DC)
    m["WDTT"] = blocks(lambda k: p["Wdt"][k].T, 8, DC)
    m["WB"] = blocks(lambda k: np.broadcast_to(p["Wx"][k, 8][:, None], (DC, DC)))
    m["WCC"] = blocks(lambda k: np.broadcast_to(p["Wx"][k, 9][:, None], (DC, DC)))
    m["WOUT"] = blocks(lambda k: p["Wout"][k])
    m["PROJ"] = p["proj_w"]
    m["FC2"][:R1] = p["fc2_w"]
    vecs = np.zeros((128, len(VECS)), f32)
    for i, n in enumerate(VECS):
        if n == "skip":
            vecs[:, i] = p["skip_scale"][0]
        elif n == "eps_in":
            vecs[:, i] = 1e-5 * 1e-6
        elif n == "eps_ln":
            vecs[:, i] = 1e-5
        else:
            flat = p[n].reshape(-1)
            vecs[:len(flat), i] = flat
    winx = np.tile(p["Win"][:, :, :DC].transpose(1, 0, 2), (3, 1, 1))
    taps = p["conv_w"][:, :, 0].transpose(2, 0, 3, 1)
    convw = np.repeat(taps, DC, axis=0)
    arrays = {
        "x": w["x"].reshape(B, C, L),
        "mats": np.stack([m[n] for n in MATS], axis=1),
        "vecs": vecs,
        "fc1": p["fc1_w"],
        "gate": f["gate_weight"],
        "winx": winx,
        "convw": convw,
        "w1": f["w1"].transpose(1, 0, 2),
        "b1": f["b1"].T,
        "w2": f["w2"].transpose(1, 0, 2),
        "b2": f["b2"],
    }
    arrays = {n: np.ascontiguousarray(a) for n, a in arrays.items()}
    nc = bacc.Bacc("TRN2", target_bir_lowering=False, num_devices=1)
    args = [nc.dram_tensor("in_" + n, a.shape, mybir.dt.from_np(a.dtype), kind="ExternalInput").ap()
            for n, a in arrays.items()]
    out = nc.dram_tensor("out", (B, C, L), F32, kind="ExternalOutput").ap()
    build_program(nc, *args, out)
    r = run(nc, [{"in_" + n: a for n, a in arrays.items()}], core_ids=[0])
    return r.results[0]["out"].reshape(B, C, HH, WW)
```

```python
from contextlib import ExitStack

import concourse.bass as bass
from concourse import mybir

ALU = mybir.AluOpType
ACT = mybir.ActivationFunctionType
AX_X = mybir.AxisListType.X
F32 = mybir.dt.float32
F32R = mybir.dt.float32r
U32 = mybir.dt.uint32

B, C, HH, WW = 16, 128, 48, 48
L = HH * WW
KD = 4
DC = C // KD
E, DFF = 16, 128
CAP = L // E * 2
R1 = C // 16
TH = 3
TL = L // TH
CH = TL // 2
CR = CH // WW
PW = WW + 2
PL = (HH + 2) * PW
SL = HH * PW
QL = L // 4
QH = QL // 2
NT = 6
TT = QL // NT
BG = 128 // E
SOFTPLUS_MAX = 40.0

MATS = ["J128", "CEN128", "CEN32", "J32", "IDENT", "WZ", "WXT", "WDTT", "WB", "WCC", "WOUT", "PROJ", "FC2"]
VECS = ["norm_w", "norm_b", "conv_b", "dt_bias", "A_log", "Dp", "onorm_w", "onorm_b", "proj_b", "fc1_b", "fc2_b",
        "skip", "eps_in", "eps_ln"]


def build_program(nc, x, mats, vecs, fc1, gate, winx, convw, w1, b1, w2, b2, out):
    x2_dram = nc.dram_tensor("x2_dram", (B, C, L), F32).ap()
    xf_parts = [nc.dram_tensor(f"xf_{n}", (B, C, L), F32).ap() for n in ("high", "low")]
    aff_dram = nc.dram_tensor("aff_dram", (B, E, L), F32).ap()
    gates_dram = nc.dram_tensor("gates_dram", (B, E, L), F32).ap()
    gate_parts = [nc.dram_tensor(f"gates_{n}", (B, E, L), F32).ap() for n in ("high", "low")]
    with ExitStack() as keep:
        def sb(name, shape, dt=F32):
            return keep.enter_context(nc.sbuf_tensor(name, shape, dt))

        psum = keep.enter_context(nc.psum_tensor("psum", [128, 8, 512], F32))
        route = Route(sb, keep.enter_context(nc.semaphore("search0")))
        mixer_phase(nc, psum, route, x, mats, vecs, fc1, gate, winx, convw, x2_dram, xf_parts, aff_dram, gates_dram, gate_parts)
        expert_phase(nc, psum, route, w1, w2, b1, b2, x2_dram, xf_parts, aff_dram, gates_dram, gate_parts, out)


def wait(eng, semaphore, value):
    if not isinstance(value, int) or value > 0:
        eng.wait_ge(semaphore, value)


def slot(psum, s):
    return psum[:, 2 * s:2 * s + 2, 0:CH]


def third(t):
    return slice(t * TL, (t + 1) * TL)


def halves(ap):
    return ap.rearrange("p (a n) -> p a n", a=2)


def done(b, t=TH - 1):
    return b * TH + (t + 1)


def in_order(k, image, c):
    if k % 2:
        image = image[:, ::-1, ::-1]
    if k >= 2:
        image = image.rearrange("p h w -> p w h")
    return image[:, c * CR:(c + 1) * CR, :]


class Route:

    BITS = 30
    STEP, INIT = 5, 2

    def __init__(self, sb, steps):
        self.steps = steps
        self.A = sb("affinities", [128, L])
        self.thr, self.cand, self.take, self.bit = (sb(n, [128, 1], U32) for n in ("thr", "cand", "take", "bit"))
        self.cnt = sb("cnt", [128, 1])

    def init(self, v, step):
        v.memset(self.thr[:], 0).then_inc(step, 1)
        v.memset(self.bit[:], 2 ** (self.BITS - 1)).then_inc(step, 1)

    def search(self, v, step, n, reached):
        base = n * self.STEP + self.INIT
        v.wait_ge(step, base)
        v.tensor_tensor(self.cand[:], self.thr[:], self.bit[:], ALU.bitwise_or).then_inc(step, 1)
        v.wait_ge(step, base + 1)
        v.tensor_scalar(reached, self.A[:], self.cand[:].bitcast(F32), 0.0, ALU.is_ge, ALU.add,
                        accum_out=self.cnt[:]).then_inc(step, 1)
        v.wait_ge(step, base + 2)
        v.tensor_scalar(self.take[:], self.cnt[:], float(CAP), self.bit[:], ALU.is_ge, ALU.mult).then_inc(step, 1)
        v.wait_ge(step, base + 3)
        v.tensor_tensor(self.thr[:], self.thr[:], self.take[:], ALU.bitwise_or).then_inc(step, 1)
        v.tensor_scalar(self.bit[:], self.bit[:], 1, None, ALU.logical_shift_right).then_inc(step, 1)

    def gates(self, v, step, stages, W, Q, gated):
        A, cnt, t = self.A[:], self.cnt[:], self.thr[:].bitcast(F32)
        n = self.INIT + self.BITS * self.STEP
        for stage in stages:
            if stage == 0:
                v.wait_ge(step, n)
                v.tensor_scalar(W, A, t, 0.0, ALU.is_gt, ALU.add, accum_out=cnt).then_inc(step, 1)
            elif stage == 1:
                v.wait_ge(step, n + 1)
                v.tensor_scalar(cnt, cnt, -1.0, float(CAP), ALU.mult, ALU.add).then_inc(step, 1)
                v.tensor_scalar(Q, A, t, None, ALU.is_equal).then_inc(step, 1)
            elif stage == 2:
                v.wait_ge(step, n + 3)
                v.tensor_tensor_scan(W, Q, Q, 0.0, ALU.add, ALU.max).then_inc(step, 1)
            elif stage == 3:
                v.wait_ge(step, n + 4)
                v.scalar_tensor_tensor(Q, W, cnt, Q, ALU.is_le, ALU.mult).then_inc(step, 1)
            elif stage == 4:
                v.wait_ge(step, n + 5)
                v.scalar_tensor_tensor(Q, A, t, Q, ALU.is_gt, ALU.add).then_inc(step, 1)
            elif stage == 5:
                v.wait_ge(step, n + 6)
                v.tensor_tensor(W, A, Q, ALU.mult).then_inc(step, 1)
            elif stage == 6:
                v.wait_ge(step, n + 7)
                v.tensor_copy(Q.bitcast(F32R), W).then_inc(step, 1)
            else:
                v.wait_ge(step, n + 8)
                v.tensor_tensor(self.A[:].bitcast(F32R), W, Q, ALU.subtract).then_inc(gated, 1)

    def store_gates(self, sp, group, W, Q, gates_dram, gate_parts, stored):
        images = slice(group * BG, (group + 1) * BG)
        for dst, src in ((gates_dram, W), (gate_parts[0], Q), (gate_parts[1], self.A[:])):
            sp.dma_start(dst[images].rearrange("b e n -> (b e) n"), src).then_inc(stored, 16)


def mixer_phase(nc, psum, route, x, mats, vecs, fc1, gate, winx, convw, x2_dram, xf_parts, aff_dram, gates_dram,
                gate_parts):
    SEARCH_FROM = 10
    PER = route.BITS // (B - 1 - SEARCH_FROM)
    with ExitStack() as ctx:
        def sb(name, shape):
            return ctx.enter_context(nc.sbuf_tensor(name, shape, F32))

        def sem(name):
            return ctx.enter_context(nc.semaphore(name))

        m_all = sb("m_all", [128, len(MATS), 128])
        M = {n: m_all[:, i, :] for i, n in enumerate(MATS)}
        v_all = sb("v_all", [128, len(VECS)])
        V = {n: v_all[:, i:i + 1] for i, n in enumerate(VECS)}
        fc1s = sb("fc1s", [128, R1])
        gates = sb("gates", [128, 32])
        winxs = sb("winxs", [96, KD, DC])
        convws = sb("convws", [96, KD, 3, DC])
        wconv = sb("wconv", [96, KD, 3, DC])
        wdelta = sb("wdelta", [128, 128])
        projw = sb("projw", [128, 128])
        projc = sb("projc", [128, 128])
        vx = sb("vx", [128, 4])
        a_neg, fc2_neg, proj_c, a_exp = (vx[:, i:i + 1] for i in range(4))

        X = [sb(f"X{i}", [128, L]) for i in range(2)]
        XS = [sb(f"XS{i}", [128, PL]) for i in range(2)]
        zsum = [sb(f"zsum{i}", [128, TH]) for i in range(2)]
        stack = sb("stack", [96, KD, SL])
        SQ = sb("SQ", [128, L])
        RS = sb("RS", [128, L])
        U = sb("U", [128, L])
        ZS = sb("ZS", [128, L])
        CLXM = sb("CLXM", [128, L])
        DH = sb("DH", [128, L])
        DA = sb("DA", [128, L])
        DU = sb("DU", [128, L])
        G = sb("G", [128, L])
        XF = G
        XF_HIGH, XF_LOW = (buf[:].bitcast(F32R) for buf in (ZS, DU))
        X2 = sb("X2", [128, L])
        se1 = sb("se1", [R1, 1])
        sex = sb("sex", [128, 1])
        s1 = sb("s1", [128, 3])
        LGT = sb("LGT", [128, QL])
        lg = sb("lg", [TT, NT, 4, E])
        aff = sb("aff", [TT, NT, 4, 32])
        lgst = sb("lgst", [TT, 3, NT, 4])

        names = ("consts a_loaded gates_ready gates_stored border_zero prep_exp prep_vec prep_mm prep_done x_loaded stacked x2_stored high_stored low_stored aff_stored "
                 "cen1_pe sq1 var1_pe ln1 rstd1 xn xs "
                 "conv_pe u z_pe zs fc1_pe relu1 fc2_pe sex_exp se_add se_done "
                 "pre_pe clamped sp_exp sp_ln delta du_pool decay bc_pe dbu cc_pe h hc "
                 "yc_pe sq2 var2_pe ln2 rstd2 yn g "
                 "out_pe xm cen3_pe sq3 var3_pe ln3 rstd3 proj_pe pr x2 "
                 "cen4_pe sq4 var4_pe ln4 rstd4 xf xf_high xf_low "
                 "skipped dpu_pool dpu lg_pe lg_copy lgt_pe lg_max lg_sub lg_exp lg_sum lg_rec aff_ready afft_pe afft").split()
        S = {n: sem("m_" + n) for n in names}
        search = route.steps

        def run(eng, front, mid, tail, gate_of_last=None, begin_search=None):
            def pair(b0, searching, ends=False):
                for par in range(2):
                    b = b0 + par
                    last = ends and par == 1
                    mid(b, par, searching)
                    if not last:
                        front(b + 1, 1 - par)
                    tail(b, par, last, searching)

            front(0, 0)
            pair(0, False)
            if begin_search:
                with eng.Fori(1, SEARCH_FROM // 2) as i:
                    pair(i * 2, False)
                begin_search()
            with eng.Fori(SEARCH_FROM // 2 if begin_search else 1, B // 2 - 1) as i:
                pair(i * 2, True)
            pair(B - 2, True, ends=True)
            if gate_of_last:
                gate_of_last()

        def after_first(b):
            return not (isinstance(b, int) and b == 0)

        block = ctx.enter_context(nc.Block())

        @block.sync
        def _(sp):
            for dst, src in ((m_all[:], mats), (v_all[:], vecs), (fc1s[:], fc1), (gates[:, 0:E], gate),
                             (winxs[:], winx), (convws[:], convw)):
                sp.dma_start(dst, src).then_inc(S["consts"], 16)

            def load(b, par):
                sp.dma_start(X[par][:], x[b]).then_inc(S["x_loaded"], 16)

            def front(b, par):
                wait(sp, S["xs"], done(b))
                wait(sp, S["conv_pe"], b * TH)
                for j in range(3):
                    for k in range(KD):
                        sp.dma_start(stack[DC * j:DC * j + DC, k, :],
                                     XS[par][DC * k:DC * k + DC, j * PW:j * PW + SL]).then_inc(S["stacked"], 16)

            def mid(b, par, searching):
                if not (isinstance(b, int) and b == B - 1):
                    wait(sp, S["x2"], b * TH)
                    load(b + 1, 1 - par)
                if after_first(b):
                    store_affinities(b)

            def tail(b, par, last, searching):
                wait(sp, S["x2"], done(b))
                sp.dma_start(x2_dram[b], X2[:]).then_inc(S["x2_stored"], 16)
                wait(sp, S["xf_high"], done(b))
                sp.dma_start(xf_parts[0][b], ZS[:]).then_inc(S["high_stored"], 16)
                wait(sp, S["xf_low"], done(b))
                sp.dma_start(xf_parts[1][b], DU[:]).then_inc(S["low_stored"], 16)

            def store_affinities(b):
                wait(sp, S["afft"], b)
                for j in range(4):
                    sp.dma_start(aff_dram[b - 1, :, j * QL:(j + 1) * QL],
                                 LGT[32 * j:32 * j + E, :]).then_inc(S["aff_stored"], 16)

            def begin_search():
                wait(sp, S["aff_stored"], 64 * (SEARCH_FROM - 1))
                sp.dma_start(route.A[:], aff_dram[0:BG].rearrange("b e n -> (b e) n")).then_inc(S["a_loaded"], 16)

            load(0, 0)
            def gate_of_last():
                wait(sp, S["gates_ready"], 1)
                route.store_gates(sp, 0, XS[B % 2][:, 0:L], X[B % 2][:], gates_dram, gate_parts, S["gates_stored"])
                store_affinities(B)

            run(sp, front, mid, tail, gate_of_last, begin_search)
            for s in ("x2_stored", "high_stored", "low_stored"):
                wait(sp, S[s], 16 * B)
            wait(sp, S["aff_stored"], 64 * B)
            wait(sp, S["gates_stored"], 16 * 3)

        @block.gpsimd
        def _(pool):
            for i in range(2):
                nc.gpsimd.memset(XS[i][:], 0.0).then_inc(S["border_zero"], 1)
            nc.gpsimd.memset(aff[:], 0.0).then_inc(S["border_zero"], 1)
            nc.gpsimd.memset(gates[:, E:32], 0.0).then_inc(S["border_zero"], 1)

            def front(b, par):
                pass

            def mid(b, par, searching):
                wait(pool, S["low_stored"], b * 16)
                for t in range(TH):
                    wait(pool, S["delta"], done(b, t))
                    wait(pool, S["u"], done(b, t))
                    nc.gpsimd.tensor_tensor(DU[:, third(t)], DH[:, third(t)], U[:, third(t)],
                                            ALU.mult).then_inc(S["du_pool"], 1)
                for t in range(TH - 1):
                    wait(pool, S["hc"], done(b, t))
                    wait(pool, S["skipped"], b * (TH - 1) + (t + 1))
                    nc.gpsimd.tensor_tensor(DU[:, third(t)], DU[:, third(t)], CLXM[:, third(t)],
                                            ALU.add).then_inc(S["dpu_pool"], 1)

            def tail(b, par, last, searching):
                wait(pool, S["yc_pe"], done(b))
                for t in range(TH):
                    wait(pool, S["xf"], done(b, t))
                    wait(pool, S["xf_high"], done(b, t))
                    nc.gpsimd.tensor_tensor(XF_LOW[:, third(t)], XF[:, third(t)], ZS[:, third(t)],
                                            ALU.subtract).then_inc(S["xf_low"], 1)

            run(pool, front, mid, tail)

        @block.scalar
        def _(act):
            def rstd(ln, ps, b, t, out_sem, eps, scale=1.0):
                nc.scalar.activation(halves(RS[:, third(t)]), slot(psum, ps), ACT.Ln, bias=V[eps],
                                     scale=scale).then_inc(S[ln], 1)
                wait(act, S[ln], done(b, t))
                nc.scalar.activation(RS[:, third(t)], RS[:, third(t)], ACT.Exp, scale=-0.5).then_inc(S[out_sem], 1)

            act.preload_act_table_set("natural_log_exp_and_others")
            wait(act, S["consts"], 16 * 6)
            nc.scalar.activation(a_exp, V["A_log"], ACT.Exp).then_inc(S["prep_exp"], 1)
            wait(act, S["prep_done"], 3)
            wait(act, S["border_zero"], 4)

            def norm(squares, rstds):
                squares(0)
                squares(1)
                rstds(0)
                squares(2)
                rstds(1)
                rstds(2)

            def front(b, par):
                def squares(t):
                    wait(act, S["cen1_pe"], done(b, t))
                    if after_first(b):
                        wait(act, S["var2_pe"], done(b - 1, t))
                    nc.scalar.activation(halves(SQ[:, third(t)]), slot(psum, 1 + t), ACT.Square).then_inc(S["sq1"], 1)

                def rstds(t):
                    wait(act, S["var1_pe"], done(b, t))
                    if after_first(b):
                        wait(act, S["yn"], done(b - 1, t))
                    rstd("ln1", 0, b, t, "rstd1", "eps_in", 1.0 + 1e-5)

                norm(squares, rstds)
                for t in range(TH):
                    wait(act, S["xn"], done(b, t))
                    view = XS[par][:].rearrange("p (h w) -> p h w", w=PW)[:, 1 + 16 * t:17 + 16 * t, 1:1 + WW]
                    nc.scalar.activation(view, view, ACT.Identity, bias=V["norm_b"],
                                         accum_out=zsum[par][:, t:t + 1]).then_inc(S["xs"], 1)

            def copy_logits(b):
                wait(act, S["lg_pe"], b)
                wait(act, S["aff_stored"], (b - 1) * 64)
                nc.scalar.activation(LGT[:].rearrange("p (a n) -> p a n", a=2), psum[:, 4:6, 0:QH],
                                     ACT.Copy).then_inc(S["lg_copy"], 1)

            def exp_logits(b):
                wait(act, S["lg_sub"], b)
                nc.scalar.activation(lg[:], lg[:], ACT.Exp).then_inc(S["lg_exp"], 1)

            def copy_affinities(b):
                wait(act, S["afft_pe"], b)
                nc.scalar.activation(LGT[:].rearrange("p (a n) -> p a n", a=2), psum[:, 4:6, 0:QH],
                                     ACT.Copy).then_inc(S["afft"], 1)

            def mid(b, par, searching):
                wait(act, S["yc_pe"], b * TH)
                for t in range(TH):
                    wait(act, S["conv_pe"], done(b, t))
                    nc.scalar.activation(halves(U[:, third(t)]), slot(psum, t), ACT.Silu,
                                         bias=V["conv_b"]).then_inc(S["u"], 1)
                wait(act, S["high_stored"], b * 16)
                wait(act, S["xf_low"], b * TH)
                for t in range(TH):
                    wait(act, S["z_pe"], done(b, t))
                    nc.scalar.activation(halves(ZS[:, third(t)]), slot(psum, (3, 0, 1)[t]),
                                         ACT.Silu).then_inc(S["zs"], 1)
                act.preload_act_table_set("natural_log_exp_and_others")
                if after_first(b):
                    copy_logits(b)
                for t in range(TH):
                    wait(act, S["clamped"], done(b, t))
                    nc.scalar.activation(CLXM[:, third(t)], CLXM[:, third(t)], ACT.Exp).then_inc(S["sp_exp"], 1)
                    wait(act, S["sp_exp"], done(b, t))
                    nc.scalar.activation(CLXM[:, third(t)], CLXM[:, third(t)], ACT.Ln, bias=1.0).then_inc(S["sp_ln"], 1)
                def decay(t):
                    wait(act, S["delta"], done(b, t))
                    nc.scalar.activation(DA[:, third(t)], DH[:, third(t)], ACT.Exp, scale=a_neg).then_inc(S["decay"], 1)

                def skipped(t):
                    nc.scalar.activation(CLXM[:, third(t)], U[:, third(t)], ACT.Copy, scale=V["Dp"]).then_inc(S["skipped"], 1)

                wait(act, S["fc1_pe"], b + 1)
                nc.scalar.activation(se1[:], psum[0:R1, 4, 0:1], ACT.Relu, bias=V["fc1_b"][0:R1],
                                     scale=1.0 / L).then_inc(S["relu1"], 1)
                wait(act, S["h"], b * TH)
                decay(0)
                wait(act, S["fc2_pe"], b + 1)
                nc.scalar.activation(sex[:], psum[:, 4, 0:1], ACT.Exp, bias=fc2_neg, scale=-1.0).then_inc(S["sex_exp"], 1)
                if after_first(b):
                    exp_logits(b)
                decay(1)
                skipped(0)
                decay(2)
                skipped(1)
                wait(act, S["var4_pe"], b * TH)
                wait(act, S["xf"], b * TH)

                def squares(t):
                    if t == 1 and after_first(b):
                        copy_affinities(b)
                    wait(act, S["yc_pe"], done(b, t))
                    nc.scalar.activation(halves(SQ[:, third(t)]), slot(psum, 1 + t), ACT.Square).then_inc(S["sq2"], 1)

                def rstds(t):
                    wait(act, S["var2_pe"], done(b, t))
                    rstd("ln2", 0, b, t, "rstd2", "eps_ln")

                norm(squares, rstds)

            def tail(b, par, last, searching):
                for t in range(TH):
                    wait(act, S["cen3_pe"], done(b, t))
                    wait(act, *((S["var2_pe"], done(b, t)) if last else (S["var1_pe"], done(b + 1, t))))
                    nc.scalar.activation(halves(SQ[:, third(t)]), slot(psum, t), ACT.Square).then_inc(S["sq3"], 1)
                for t in range(TH):
                    wait(act, S["var3_pe"], done(b, t))
                    wait(act, *((S["yn"], done(b, t)) if last else (S["xn"], done(b + 1, t))))
                    rstd("ln3", (3, 0, 1)[t], b, t, "rstd3", "eps_ln")

                def squares(t):
                    wait(act, S["cen4_pe"], done(b, t))
                    wait(act, S["var3_pe"], done(b, t))
                    nc.scalar.activation(halves(SQ[:, third(t)]), slot(psum, 1 + t), ACT.Square).then_inc(S["sq4"], 1)

                def rstds(t):
                    wait(act, S["var4_pe"], done(b, t))
                    wait(act, S["pr"], done(b, t))
                    rstd("ln4", 0, b, t, "rstd4", "eps_ln")

                norm(squares, rstds)
                wait(act, S["g"], done(b))
                for t in range(TH):
                    wait(act, S["xf"], done(b, t))
                    nc.scalar.activation(XF_HIGH[:, third(t)], XF[:, third(t)], ACT.Copy).then_inc(S["xf_high"], 1)

            def gate_of_last():
                copy_logits(B)
                exp_logits(B)
                copy_affinities(B)

            run(act, front, mid, tail, gate_of_last)

        @block.vector
        def _(dve):
            v = nc.vector
            wait(dve, S["consts"], 16 * 6)
            for dx in range(3):
                v.tensor_tensor(wconv[:, :, dx, :], winxs[:], convws[:, :, dx, :], ALU.mult).then_inc(S["prep_vec"], 1)
            v.tensor_scalar(projw[:], M["PROJ"], V["norm_w"], None, ALU.mult).then_inc(S["prep_vec"], 1)
            v.tensor_scalar(fc2_neg, V["fc2_b"], -1.0, None, ALU.mult).then_inc(S["prep_vec"], 1)
            wait(dve, S["prep_exp"], 1)
            v.tensor_scalar(a_neg, a_exp, -1.0, None, ALU.mult).then_inc(S["prep_vec"], 1)
            wait(dve, S["prep_mm"], 3)
            v.tensor_copy(wdelta[:], psum[:, 0, 0:128]).then_inc(S["prep_done"], 1)
            v.tensor_copy(projc[:], psum[:, 2, 0:128]).then_inc(S["prep_done"], 1)
            v.tensor_tensor(proj_c, psum[:, 4, 0:1], V["proj_b"], ALU.add).then_inc(S["prep_done"], 1)
            wait(dve, S["prep_vec"], 6)
            wait(dve, S["prep_done"], 3)
            wait(dve, S["border_zero"], 4)

            def interior(par, t):
                return XS[par][:].rearrange("p (h w) -> p h w", w=PW)[:, 1 + 16 * t:17 + 16 * t, 1:1 + WW]

            def rows(ap):
                return ap.rearrange("p (a h w) -> p a h w", a=2, w=WW)

            def ps_rows(s):
                return slot(psum, s).rearrange("p a (h w) -> p a h w", w=WW)

            def front(b, par):
                for t in range(TH):
                    wait(dve, S["rstd1"], done(b, t))
                    v.scalar_tensor_tensor(interior(par, t).rearrange("p (a h) w -> p a h w", a=2), ps_rows(1 + t),
                                           V["norm_w"], rows(RS[:, third(t)]), ALU.mult, ALU.mult).then_inc(S["xn"], 1)

            def mid(b, par, searching):
                if searching:
                    find_gates(b, par, range(0, 3))
                wait(dve, S["proj_pe"], b * TH)
                for t in range(TH):
                    wait(dve, S["pre_pe"], done(b, t))
                    v.tensor_scalar(halves(CLXM[:, third(t)]), slot(psum, (3, 0, 1)[t]), V["dt_bias"], SOFTPLUS_MAX,
                                    ALU.add, ALU.min).then_inc(S["clamped"], 1)
                if after_first(b):
                    shift_logits(b)
                wait(dve, S["yc_pe"], b * TH)
                def delta(t):
                    wait(dve, S["sp_ln"], done(b, t))
                    v.scalar_tensor_tensor(halves(DH[:, third(t)]), slot(psum, (3, 0, 1)[t]), V["dt_bias"],
                                           halves(CLXM[:, third(t)]), ALU.add, ALU.max).then_inc(S["delta"], 1)

                def dbu(t):
                    wait(dve, S["bc_pe"], done(b, t))
                    wait(dve, S["du_pool"], done(b, t))
                    v.tensor_tensor(halves(DU[:, third(t)]), halves(DU[:, third(t)]), slot(psum, (3, 0, 1)[t]),
                                    ALU.mult).then_inc(S["dbu"], 1)

                def scan(t):
                    wait(dve, S["decay"], done(b, t))
                    wait(dve, S["dbu"], done(b, t))
                    if t:
                        wait(dve, S["h"], done(b, t - 1))
                    v.tensor_tensor_scan(DH[:, third(t)], DA[:, third(t)], DU[:, third(t)],
                                         DH[:, t * TL - 1:t * TL] if t else 0.0, ALU.mult, ALU.add).then_inc(S["h"], 1)

                def hc(t):
                    wait(dve, S["cc_pe"], done(b, t))
                    wait(dve, S["h"], done(b, t))
                    v.tensor_tensor(halves(DU[:, third(t)]), halves(DH[:, third(t)]), slot(psum, (2, 3, 0)[t]),
                                    ALU.mult).then_inc(S["hc"], 1)

                delta(0)
                delta(1)
                dbu(0)
                delta(2)
                scan(0)
                dbu(1)
                hc(0)
                if after_first(b):
                    affinities(b)
                scan(1)
                dbu(2)
                hc(1)
                scan(2)
                hc(2)
                wait(dve, S["hc"], done(b))
                v.scalar_tensor_tensor(DU[:, third(TH - 1)], U[:, third(TH - 1)], V["Dp"], DU[:, third(TH - 1)],
                                       ALU.mult, ALU.add).then_inc(S["dpu"], 1)
                wait(dve, S["sex_exp"], b + 1)
                wait(dve, S["xm"], b * TH)
                v.tensor_scalar(s1[:, 0:1], sex[:], 1.0, None, ALU.add).then_inc(S["se_add"], 1)
                wait(dve, S["se_add"], b * 2 + 1)
                v.reciprocal(s1[:, 1:2], s1[:, 0:1]).then_inc(S["se_add"], 1)
                wait(dve, S["se_add"], b * 2 + 2)
                v.tensor_tensor(s1[:, 2:3], s1[:, 1:2], V["skip"], ALU.mult).then_inc(S["se_done"], 1)
                wait(dve, S["xf_low"], b * TH)
                wait(dve, S["lg_pe"], b)
                for t in range(TH):
                    wait(dve, S["rstd2"], done(b, t))
                    v.scalar_tensor_tensor(halves(G[:, third(t)]), slot(psum, 1 + t), V["onorm_w"], halves(RS[:, third(t)]),
                                           ALU.mult, ALU.mult).then_inc(S["yn"], 1)
                    wait(dve, S["yn"], done(b, t))
                    wait(dve, S["zs"], done(b, t))
                    v.scalar_tensor_tensor(G[:, third(t)], G[:, third(t)], V["onorm_b"], ZS[:, third(t)],
                                           ALU.add, ALU.mult).then_inc(S["g"], 1)
                if searching:
                    find_gates(b, par, range(3, 4))

            def tail(b, par, last, searching):
                wait(dve, S["se_done"], b + 1)
                for t in range(TH):
                    wait(dve, S["out_pe"], done(b, t))
                    v.scalar_tensor_tensor(rows(CLXM[:, third(t)]), interior(par, t).rearrange("p (a h) w -> p a h w", a=2),
                                           s1[:, 2:3], ps_rows(1 + t), ALU.mult, ALU.mult).then_inc(S["xm"], 1)
                if searching:
                    find_gates(b, par, range(4, 5))
                wait(dve, S["x2_stored"], b * 16)
                wait(dve, S["cen4_pe"], b * TH)
                for t in range(TH):
                    wait(dve, S["proj_pe"], done(b, t))
                    wait(dve, S["rstd3"], done(b, t))
                    v.tensor_tensor(halves(X2[:, third(t)]), slot(psum, (2, 3, 0)[t]), halves(RS[:, third(t)]),
                                    ALU.mult).then_inc(S["pr"], 1)
                    wait(dve, S["pr"], done(b, t))
                    v.scalar_tensor_tensor(X2[:, third(t)], X2[:, third(t)], proj_c, X[par][:, third(t)],
                                           ALU.add, ALU.add).then_inc(S["x2"], 1)
                if searching:
                    find_gates(b, par, range(5, PER + 2 * (isinstance(b, int) and b == B - 1)))
                wait(dve, S["out_pe"], done(b))
                for t in range(TH):
                    wait(dve, S["rstd4"], done(b, t))
                    v.tensor_tensor(halves(XF[:, third(t)]), slot(psum, 1 + t), halves(RS[:, third(t)]),
                                    ALU.mult).then_inc(S["xf"], 1)

            def banks(ap):
                return ap.rearrange("p (a i) j -> p a (i j)", a=2)

            def shift_logits(b):
                wait(dve, S["lgt_pe"], b)
                lp = psum[0:TT, 4:6, 0:NT // 2 * 128].rearrange("p a (g e) -> p a g e", e=32)[:, :, :, 0:E]
                v.tensor_reduce(banks(lgst[:, 0]), lp, AX_X, ALU.max).then_inc(S["lg_max"], 1)
                wait(dve, S["lg_max"], b)
                v.tensor_tensor(lg[:].rearrange("p (a i) j e -> p a (i j) e", a=2), lp,
                                banks(lgst[:, 0]).unsqueeze(3).to_broadcast([TT, 2, NT * 2, E]),
                                ALU.subtract).then_inc(S["lg_sub"], 1)

            def affinities(b):
                wait(dve, S["lg_exp"], b)
                v.tensor_reduce(lgst[:, 1], lg[:], AX_X, ALU.add).then_inc(S["lg_sum"], 1)
                wait(dve, S["lg_sum"], b)
                v.reciprocal(lgst[:, 2], lgst[:, 1]).then_inc(S["lg_rec"], 1)
                wait(dve, S["lg_rec"], b)
                wait(dve, S["afft_pe"], b - 1)
                v.tensor_tensor(aff[:, :, :, 0:E], lg[:], lgst[:, 2].unsqueeze(3).to_broadcast([TT, NT, 4, E]),
                                ALU.mult).then_inc(S["aff_ready"], 1)

            def begin_search():
                route.init(v, search)
                wait(dve, S["a_loaded"], 16)

            def find_gates(b, par, stages):
                if isinstance(b, int) and b == B - 1:
                    route.gates(v, search, stages, XS[1 - par][:, 0:L], X[1 - par][:], S["gates_ready"])
                else:
                    for n in stages:
                        route.search(v, search, (b - SEARCH_FROM) * PER + n, DA[:])

            def gate_of_last():
                shift_logits(B)
                affinities(B)

            run(dve, front, mid, tail, gate_of_last, begin_search)

        @block.tensor
        def _(pe):
            mm = nc.tensor.matmul

            def full(s, w, src, t):
                for a in range(2):
                    last = mm(psum[:, 2 * s + a, 0:CH], w, src[:, t * TL + a * CH:t * TL + (a + 1) * CH],
                              start=True, stop=True)
                return last

            wait(pe, S["consts"], 16 * 6)
            wait(pe, S["prep_vec"], 6)
            mm(psum[:, 0, 0:128], M["WXT"][0:32], M["WDTT"][0:32], start=True, stop=True).then_inc(S["prep_mm"], 1)
            mm(psum[:, 2, 0:128], M["CEN128"], projw[:], start=True, stop=True).then_inc(S["prep_mm"], 1)
            mm(psum[:, 4, 0:1], M["PROJ"], V["norm_b"], start=True, stop=True).then_inc(S["prep_mm"], 1)
            wait(pe, S["prep_done"], 3)
            wait(pe, S["border_zero"], 4)

            def norm(centre, variance):
                centre(0)
                centre(1)
                variance(0)
                centre(2)
                variance(1)
                variance(2)

            def front(b, par):
                wait(pe, S["x_loaded"], b * 16 + 16)

                def centre(t):
                    if after_first(b):
                        wait(pe, S["yn"], done(b - 1, t))
                    full(1 + t, M["CEN128"], X[par], t).then_inc(S["cen1_pe"], 1)

                def variance(t):
                    wait(pe, S["sq1"], done(b, t))
                    if t:
                        wait(pe, S["ln1"], done(b, t - 1))
                    elif after_first(b):
                        wait(pe, S["ln2"], done(b - 1))
                    full(0, M["J128"], SQ, t).then_inc(S["var1_pe"], 1)

                norm(centre, variance)

            def logits(b):
                wait(pe, S["xf"], b * TH)
                for a in range(2):
                    for j in range(4):
                        at = j * QL + a * QH
                        last = mm(psum[32 * j:32 * j + 32, 4 + a, 0:QH], gates[:], XF[:, at:at + QH], start=True, stop=True)
                last.then_inc(S["lg_pe"], 1)

            def transpose_logits(b):
                wait(pe, S["lg_copy"], b)
                for n in range(NT):
                    bank, col = 4 + n // 3, n % 3 * 128
                    last = nc.tensor.transpose(psum[0:TT, bank, col:col + 128], LGT[:, n * TT:(n + 1) * TT], M["IDENT"])
                last.then_inc(S["lgt_pe"], 1)

            def transpose_affinities(b):
                wait(pe, S["aff_ready"], b)
                for n in range(NT):
                    bank, col = 4 + n // 3, n % 3 * TT
                    last = nc.tensor.transpose(psum[:, bank, col:col + TT], aff[:, n].rearrange("p j e -> p (j e)"),
                                               M["IDENT"][0:TT, 0:TT])
                last.then_inc(S["afft_pe"], 1)

            def mid(b, par, searching):
                wait(pe, S["stacked"], (b + 1) * (3 * KD * 16))
                for t in range(TH):
                    if t == 0:
                        wait(pe, S["ln4"], b * TH)
                    elif after_first(b):
                        wait(pe, S["xf"], done(b - 1, t - 1))
                    for a in range(2):
                        for dx in range(3):
                            for k in range(KD):
                                img = stack[:, k, :].rearrange("p (h w) -> p h w", w=PW)[:, :, dx:dx + WW]
                                last = mm(psum[32 * k:32 * k + 32, 2 * t + a, 0:CH], wconv[:, k, dx, :],
                                          in_order(k, img, 2 * t + a), start=(dx == 0), stop=(dx == 2))
                    last.then_inc(S["conv_pe"], 1)
                for t in range(TH):
                    s = (3, 0, 1)[t]
                    if t == 0:
                        wait(pe, S["xf"], b * TH)
                    else:
                        wait(pe, S["u"], done(b, t - 1))
                    for a in range(2):
                        for k in range(KD):
                            img = XS[par][:].rearrange("p (h w) -> p h w", w=PW)[:, 1:1 + HH, 1:1 + WW]
                            last = mm(psum[32 * k:32 * k + 32, 2 * s + a, 0:CH], M["WZ"][:, 32 * k:32 * k + 32],
                                      in_order(k, img, 2 * t + a), start=True, stop=True)
                    last.then_inc(S["z_pe"], 1)
                wait(pe, S["u"], done(b))
                if after_first(b):
                    logits(b)
                for t in range(TH):
                    wait(pe, S["zs"], done(b, t))
                    full((3, 0, 1)[t], wdelta[:], U, t).then_inc(S["pre_pe"], 1)
                if after_first(b):
                    transpose_logits(b)
                wait(pe, S["lg_sub"], b)
                for n in range(TH):
                    last = mm(psum[0:R1, 4, 0:1], fc1s[:], zsum[par][:, n:n + 1], start=(n == 0), stop=(n == TH - 1))
                last.then_inc(S["fc1_pe"], 1)
                def spread_b(t):
                    wait(pe, S["delta"], done(b, t))
                    full((3, 0, 1)[t], M["WB"], U, t).then_inc(S["bc_pe"], 1)

                def spread_c(t):
                    if t == 0:
                        wait(pe, S["sex_exp"], b + 1)
                    else:
                        wait(pe, S["dbu"], done(b, t - 1))
                    full((2, 3, 0)[t], M["WCC"], U, t).then_inc(S["cc_pe"], 1)

                spread_b(0)
                wait(pe, S["relu1"], b + 1)
                mm(psum[:, 4, 0:1], M["FC2"][0:R1], se1[:], start=True, stop=True).then_inc(S["fc2_pe"], 1)
                spread_b(1)
                spread_c(0)
                spread_b(2)
                spread_c(1)
                spread_c(2)

                def centre(t):
                    if t == 0:
                        wait(pe, S["dbu"], done(b))
                    if t == 1 and after_first(b):
                        transpose_affinities(b)
                        wait(pe, S["afft"], b)
                    if t < TH - 1:
                        wait(pe, S["dpu_pool"], b * (TH - 1) + (t + 1))
                    else:
                        wait(pe, S["dpu"], b + 1)
                    full(1 + t, M["CEN32"], DU, t).then_inc(S["yc_pe"], 1)

                def variance(t):
                    wait(pe, S["sq2"], done(b, t))
                    if t == 0:
                        wait(pe, S["hc"], done(b))
                    else:
                        wait(pe, S["ln2"], done(b, t - 1))
                    full(0, M["J32"], SQ, t).then_inc(S["var2_pe"], 1)

                norm(centre, variance)

            def tail(b, par, last_image, searching):
                wait(pe, S["g"], done(b))
                for t in range(TH):
                    wait(pe, *((S["yn"], done(b, t)) if last_image else (S["xn"], done(b + 1, t))))
                    for a in range(2):
                        for k in range(KD):
                            seq = G[:].rearrange("p (h w) -> p h w", w=WW)
                            last = mm(psum[32 * k:32 * k + 32, 2 * (1 + t) + a, 0:CH], M["WOUT"][:, 32 * k:32 * k + 32],
                                      in_order(k, seq, 2 * t + a), start=True, stop=True)
                    last.then_inc(S["out_pe"], 1)
                wait(pe, *((S["ln2"], done(b)) if last_image else (S["ln1"], done(b + 1))))
                for t in range(TH):
                    wait(pe, S["xm"], done(b, t))
                    full(t, M["CEN128"], CLXM, t).then_inc(S["cen3_pe"], 1)
                for t in range(TH):
                    wait(pe, S["sq3"], done(b, t))
                    full((3, 0, 1)[t], M["J128"], SQ, t).then_inc(S["var3_pe"], 1)
                for t in range(TH):
                    if t:
                        wait(pe, S["ln3"], done(b, t - 1))
                    full((2, 3, 0)[t], projc[:], CLXM, t).then_inc(S["proj_pe"], 1)

                def centre(t):
                    if t == 0:
                        wait(pe, S["ln3"], done(b))
                    wait(pe, S["x2"], done(b, t))
                    full(1 + t, M["CEN128"], X2, t).then_inc(S["cen4_pe"], 1)

                def variance(t):
                    wait(pe, S["sq4"], done(b, t))
                    if t == 0:
                        wait(pe, S["pr"], done(b))
                    else:
                        wait(pe, S["ln4"], done(b, t - 1))
                    full(0, M["J128"], SQ, t).then_inc(S["var4_pe"], 1)

                norm(centre, variance)

            def gate_of_last():
                logits(B)
                transpose_logits(B)
                wait(pe, S["lg_sub"], B)
                transpose_affinities(B)

            run(pe, front, mid, tail, gate_of_last)


def expert_phase(nc, psum, route, w1, w2, b1, b2, x2_dram, xf_parts, aff_dram, gates_dram, gate_parts, out):
    P = B // 2
    TP = 2 * TH
    UN = TP * E
    GROUP_P = BG // 2
    SEARCHED = 3
    PER = Route.BITS // SEARCHED
    LAG_PARTS = 1
    LAG_OUT = 3
    LAG_FIN = 4
    NH, NGB = 4, 4
    LOADS = 7
    R3 = 64 + E
    with ExitStack() as ctx:
        def sb(name, shape, dt=F32):
            return ctx.enter_context(nc.sbuf_tensor(name, shape, dt))

        def sem(name):
            return ctx.enter_context(nc.semaphore(name))

        w1p = [sb(f"w1p{i}", [128, E, DFF], F32R) for i in range(2)]
        w2p = [sb(f"w2p{i}", [128, E, C], F32R) for i in range(2)]
        b1s = sb("b1s", [128, E])
        b2s = sb("b2s", [R3, C])
        b2p = sb("b2p", [R3, C], F32R)
        W, Q = sb("W", [128, L]), sb("Q", [128, L])
        XFP = [[sb(f"xfp{t}_{i}", [128, TL], F32R) for i in range(2)] for t in range(TH)]
        X2 = [sb(f"x2{t}", [128, TL]) for t in range(TH)]
        GRP = [sb(f"grp{t}", [R3, TL], F32R) for t in range(TH)]
        GQ = [sb(f"gq{t}", [128, E // 4, TL]) for t in range(TH)]
        Hd_all = sb("hd_all", [128, NH, TL])
        Hd = [Hd_all[:, i, :] for i in range(NH)]
        HP = [[sb(f"hp{i}_{j}", [128, TL], F32R) for j in range(2)] for i in range(NH)]
        GB_all = sb("gb_all", [128, NGB, TL])
        GB = [GB_all[:, i, :] for i in range(NGB)]
        whole = [m[:].rearrange("p a n -> p (a n)")[:, 0:E * 128].rearrange("p (e n) -> p e n", e=E)
                 for m in (Hd_all, GB_all)]
        loaded, stored = [sem(f"e_loaded{t}") for t in range(TH)], [sem(f"e_stored{t}") for t in range(TH)]
        pool_turn = sem("e_pool_turn")
        w_loaded = [sem(f"e_w_loaded{n}") for n in range(2)]
        b_loaded, w_high, w_low, zeros, b2_high, b2_low = (
            sem("e_" + n) for n in ("b_loaded", "w_high", "w_low", "zeros", "b2_high", "b2_low"))
        a_loaded, gates_ready, gates_stored = sem("e_a_loaded"), sem("e_gates_ready"), sem("e_gates_stored")
        search1 = sem("e_search1")
        layer1, gelu, gates_spread, gated, high, low, layer2, fin = (
            sem("e_" + n) for n in ("layer1", "gelu", "gates_spread", "gated", "high", "low", "layer2", "fin"))
        block = ctx.enter_context(nc.Block())

        def units(eng, step, lag):
            for u in range(UN):
                step(0, u, False)
            with eng.Fori(1, P) as p:
                for u in range(UN):
                    step(p, u, False)
            for u in range(lag):
                step(P, u, True)

        def behind(p, u, lag):
            if u >= lag:
                return not (isinstance(p, int) and p == P), p, u - lag
            return not (isinstance(p, int) and p == 0), p - 1, u - lag + UN

        def thirds(p, th):
            return p * TP + (th + 1)

        def inputs(p, th):
            return (p * 2 + (th // TH + 1)) * (16 * LOADS)

        @block.sync
        def _(sp):
            def load(p, th):
                t, b = th % TH, p * 2 + th // TH
                for part, src in zip(XFP[t], xf_parts):
                    sp.dma_start(part[:].bitcast(F32), src[b, :, third(t)]).then_inc(loaded[t], 16)
                sp.dma_start(GQ[t][0:97:32, :, :],
                             gates_dram[b, :, third(t)].rearrange("(q j) n -> q j n", q=4)).then_inc(loaded[t], 16)
                for row, n in ((0, 0), (32, 0), (64, 1)):
                    sp.dma_start(GRP[t][row:row + E, :].bitcast(F32), gate_parts[n][b, :, third(t)]).then_inc(loaded[t], 16)
                sp.dma_start(X2[t][:], x2_dram[b, :, third(t)]).then_inc(loaded[t], 16)

            def store(p, th):
                t, b = th % TH, p * 2 + th // TH
                sp.wait_ge(fin, thirds(p, th))
                sp.dma_start(out[b, :, third(t)], X2[t][:]).then_inc(stored[t], 16)
                sp.wait_ge(stored[t], (b + 1) * 16)

            def pairs(first, end):
                with sp.Fori(first, end) as p:
                    for th in range(TP):
                        store(p, th - TH)
                        load(p, th)

            sp.dma_start(whole[0], w1).then_inc(w_loaded[0], 16)
            sp.dma_start(whole[1], w2).then_inc(w_loaded[1], 16)
            sp.dma_start(b1s[:], b1).then_inc(b_loaded, 16)
            sp.wait_ge(zeros, 1 + TH)
            for row in (0, 32, 64):
                sp.dma_start(b2s[row:row + E, :], b2).then_inc(b_loaded, 16)
            for t in range(TH):
                load(0, t)
            sp.dma_start(route.A[:], aff_dram[BG:B].rearrange("b e n -> (b e) n")).then_inc(a_loaded, 16)
            for t in range(TH):
                store(0, t)
                load(0, t + TH)
            pairs(1, GROUP_P)
            sp.wait_ge(gates_ready, 1)
            route.store_gates(sp, 1, W[:], Q[:], gates_dram, gate_parts, gates_stored)
            sp.wait_ge(gates_stored, 16 * 3)
            pairs(GROUP_P, P)
            for t in range(TH):
                store(P, t - TH)

        @block.gpsimd
        def _(pool):
            def step(p, u, late):
                th, e = divmod(u, E)
                if e == 0:
                    pool.wait_ge(loaded[th % TH], inputs(p, th))
                wait(pool, gated, p * UN + (u - NGB + 1))
                wait(pool, gates_spread, p * UN + u)
                pool.sem_inc(pool_turn, 1)
                q, j = divmod(e, 4)
                nc.gpsimd.partition_broadcast(GB[u % NGB], GQ[th % TH][32 * q:32 * q + 1, j, :]).then_inc(gates_spread, 1)

            pool.wait_ge(w_high, 2)
            nc.gpsimd.tensor_tensor(w2p[1][:], whole[1], w2p[0][:].bitcast(F32), ALU.subtract).then_inc(w_low, 1)
            pool.wait_ge(w_low, 2)
            units(pool, step, 0)

        @block.tensor
        def _(pe):
            def product(s, weights, parts, before=False, close=True):
                passes = [(0, 0), (0, 1), (1, 0)]
                for n, (i, j) in enumerate(passes):
                    for a in range(2):
                        last = nc.tensor.matmul(psum[:, 2 * s + a, 0:CH], weights[i], parts[j][:, a * CH:(a + 1) * CH],
                                                start=(n == 0 and not before), stop=(n == 2 and close))
                return last

            def step(p, u, late):
                if not late:
                    th, e = divmod(u, E)
                    if e == 0:
                        pe.wait_ge(loaded[th % TH], inputs(p, th))
                    wait(pe, gelu, p * UN + (u - 1))
                    product(u % 2, [w[:, e, :] for w in w1p], XFP[th % TH]).then_inc(layer1, 1)
                there, p, u = behind(p, u, LAG_OUT)
                if not there:
                    return
                th, e = divmod(u, E)
                s = 2 + th % 2
                if e == 0:
                    wait(pe, fin, thirds(p, th - 2))
                    for a in range(2):
                        nc.tensor.matmul(psum[:, 2 * s + a, 0:CH], b2p[:], GRP[th % TH][:, a * CH:(a + 1) * CH],
                                         start=True, stop=False)
                pe.wait_ge(low, p * UN + (u + 1))
                product(s, [w[:, e, :] for w in w2p], HP[u % NH], before=True, close=(e == E - 1)).then_inc(layer2, 1)

            pe.wait_ge(w_low, 2)
            pe.wait_ge(b2_low, 1)
            units(pe, step, LAG_OUT)

        @block.scalar
        def _(act):
            def step(p, u, late):
                if not late:
                    e = u % E
                    act.wait_ge(layer1, p * UN + (u + 1))
                    wait(act, low, p * UN + (u - NH + 1))
                    nc.scalar.activation(halves(Hd[u % NH]), slot(psum, u % 2), ACT.Gelu_apprx_tanh,
                                         bias=b1s[:, e:e + 1]).then_inc(gelu, 1)
                there, p, u = behind(p, u, LAG_PARTS)
                if not there:
                    return
                act.wait_ge(gated, p * UN + (u + 1))
                wait(act, layer2, p * UN + (u - NH + 1))
                nc.scalar.activation(HP[u % NH][0][:], Hd[u % NH], ACT.Copy).then_inc(high, 1)

            for n, parts in enumerate((w1p, w2p)):
                act.wait_ge(w_loaded[n], 16)
                nc.scalar.activation(parts[0][:], whole[n], ACT.Copy).then_inc(w_high, 1)
            act.wait_ge(b_loaded, 64)
            nc.scalar.activation(b2p[:], b2s[:], ACT.Copy).then_inc(b2_high, 1)
            act.wait_ge(w_low, 2)
            units(act, step, LAG_PARTS)

        @block.vector
        def _(dve):
            v = nc.vector

            def step(p0, u0, late):
                there, p, u = behind(p0, u0, LAG_FIN)
                if there and u % E == E - 1:
                    th = u // E
                    t = th % TH
                    dve.wait_ge(layer2, p * UN + (u + 1))
                    dve.wait_ge(loaded[t], inputs(p, th))
                    v.tensor_tensor(halves(X2[t][:]), slot(psum, 2 + th % 2), halves(X2[t][:]), ALU.add).then_inc(fin, 1)
                if not late:
                    dve.wait_ge(gelu, p0 * UN + (u0 + 1))
                    dve.wait_ge(gates_spread, p0 * UN + (u0 + 1))
                    v.tensor_tensor(Hd[u0 % NH], Hd[u0 % NH], GB[u0 % NGB], ALU.mult).then_inc(gated, 1)
                there, p, u = behind(p0, u0, LAG_PARTS)
                if there:
                    dve.wait_ge(high, p * UN + (u + 1))
                    v.tensor_tensor(HP[u % NH][1][:], Hd[u % NH], HP[u % NH][0][:].bitcast(F32),
                                    ALU.subtract).then_inc(low, 1)

            def pair(p, searching=False, gates=False):
                for u in range(UN):
                    step(p, u, False)
                    n, at = divmod(u, UN // PER)
                    if searching and at == 4 and n < PER:
                        route.search(v, search1, p * PER + n, Q[:])
                    if gates and at == 4 and n < 8:
                        route.gates(v, search1, [n], W[:], Q[:], gates_ready)

            for g in GRP:
                v.memset(g[:].bitcast(F32), 0.0).then_inc(zeros, 1)
            v.memset(b2s[:], 0.0).then_inc(zeros, 1)
            route.init(v, search1)
            dve.wait_ge(w_high, 1)
            v.tensor_tensor(w1p[1][:], whole[0], w1p[0][:].bitcast(F32), ALU.subtract).then_inc(w_low, 1)
            dve.wait_ge(b2_high, 1)
            rows = slice(32, 32 + E)
            v.tensor_tensor(b2p[rows, :], b2s[rows, :], b2p[rows, :].bitcast(F32), ALU.subtract).then_inc(b2_low, 1)
            dve.wait_ge(w_low, 2)
            dve.wait_ge(a_loaded, 16)
            pair(0, searching=True)
            with dve.Fori(1, SEARCHED) as p:
                pair(p, searching=True)
            pair(SEARCHED, gates=True)
            with dve.Fori(SEARCHED + 1, P) as p:
                pair(p)
            for u in range(LAG_FIN):
                step(P, u, True)


def kernel(**inputs):
    import numpy as np
    import concourse.bacc as bacc
    from concourse.bass_utils import run_bass_kernel_spmd as run

    w = {n: np.asarray(a) for n, a in inputs.items()}
    p = {n.removeprefix("L0_conv_"): a for n, a in w.items() if n.startswith("L0_conv_")}
    f = {n.removeprefix("L0_ffn_"): a for n, a in w.items() if n.startswith("L0_ffn_")}
    f32 = np.float32

    def blocks(of, rows=DC, cols=DC):
        m = np.zeros((128, 128), f32)
        for k in range(KD):
            m[k * rows:(k + 1) * rows, k * cols:(k + 1) * cols] = of(k)
        return m

    m = {n: np.zeros((128, 128), f32) for n in MATS}
    m["IDENT"] = np.eye(128, dtype=f32)
    m["J128"] = np.full((128, 128), 1.0 / C, f32)
    m["J32"] = blocks(lambda k: f32(1.0 / DC))
    m["CEN128"] = m["IDENT"] - m["J128"]
    m["CEN32"] = m["IDENT"] - m["J32"]
    m["WZ"] = blocks(lambda k: p["Win"][k][:, DC:])
    m["WXT"] = blocks(lambda k: p["Wx"][k, :8], 8, DC)
    m["WDTT"] = blocks(lambda k: p["Wdt"][k].T, 8, DC)
    m["WB"] = blocks(lambda k: np.broadcast_to(p["Wx"][k, 8][:, None], (DC, DC)))
    m["WCC"] = blocks(lambda k: np.broadcast_to(p["Wx"][k, 9][:, None], (DC, DC)))
    m["WOUT"] = blocks(lambda k: p["Wout"][k])
    m["PROJ"] = p["proj_w"]
    m["FC2"][:R1] = p["fc2_w"]
    vecs = np.zeros((128, len(VECS)), f32)
    for i, n in enumerate(VECS):
        if n == "skip":
            vecs[:, i] = p["skip_scale"][0]
        elif n == "eps_in":
            vecs[:, i] = 1e-5 * 1e-6
        elif n == "eps_ln":
            vecs[:, i] = 1e-5
        else:
            flat = p[n].reshape(-1)
            vecs[:len(flat), i] = flat
    winx = np.tile(p["Win"][:, :, :DC].transpose(1, 0, 2), (3, 1, 1))
    taps = p["conv_w"][:, :, 0].transpose(2, 0, 3, 1)
    convw = np.repeat(taps, DC, axis=0)
    arrays = {
        "x": w["x"].reshape(B, C, L),
        "mats": np.stack([m[n] for n in MATS], axis=1),
        "vecs": vecs,
        "fc1": p["fc1_w"],
        "gate": f["gate_weight"],
        "winx": winx,
        "convw": convw,
        "w1": f["w1"].transpose(1, 0, 2),
        "b1": f["b1"].T,
        "w2": f["w2"].transpose(1, 0, 2),
        "b2": f["b2"],
    }
    arrays = {n: np.ascontiguousarray(a) for n, a in arrays.items()}
    nc = bacc.Bacc("TRN2", target_bir_lowering=False, num_devices=1)
    args = [nc.dram_tensor("in_" + n, a.shape, mybir.dt.from_np(a.dtype), kind="ExternalInput").ap()
            for n, a in arrays.items()]
    out = nc.dram_tensor("out", (B, C, L), F32, kind="ExternalOutput").ap()
    build_program(nc, *args, out)
    r = run(nc, [{"in_" + n: a for n, a in arrays.items()}], core_ids=[0])
    return r.results[0]["out"].reshape(B, C, HH, WW)
```
